# Optimizing a Trainium2 kernel written in Bass

```python
import numpy as np
import jax
import jax.numpy as jnp

def _softmax(x, axis=-1):
    return jax.nn.softmax(x, axis=axis)

def _gelu(x):
    return jax.nn.gelu(x, approximate=True)

def _silu(x):
    return jax.nn.silu(x)

def _sigmoid(x):
    return jax.nn.sigmoid(x)

def _layernorm(x, axis=-1, eps=1e-05):
    m = jnp.mean(x, axis=axis, keepdims=True)
    v = jnp.var(x, axis=axis, keepdims=True)
    return (x - m) / jnp.sqrt(v + eps)

def _scatter_add(tgt, idx, src, axis=0):
    return tgt.at[idx].add(src)

def _segment_sum(src, seg, n):
    return jax.ops.segment_sum(src, seg, n)
kernel_name = 'mk_hybrid_d2_jaxref_r8_579e51'

def setup_inputs(seed: int=0):
    np.random.seed(seed)
    _w = jnp.asarray

    def _L0_attn_a_setup():
        import jax, jax.numpy as jnp
        import numpy as np
        HIDDEN = 128
        INNER = 256
        STATE = 64
        K = 4
        BATCH, SEQ = (2, 256)
        key = jax.random.key(seed)
        ks = jax.random.split(key, 8)

        def w(k, shape, scale=0.02):
            return jax.random.normal(k, shape, jnp.float32) * scale
        return {'x': jax.random.normal(ks[0], (BATCH, SEQ, HIDDEN), jnp.float32), 'W_in': w(ks[1], (HIDDEN, 2 * INNER)), 'conv_w': w(ks[2], (INNER, 1, K), 0.2), 'conv_b': jnp.zeros((INNER,), jnp.float32), 'W_dt': w(ks[3], (INNER, INNER)), 'b_dt': jnp.linspace(-4.0, -2.0, INNER).astype(jnp.float32), 'W_B': w(ks[4], (INNER, STATE)), 'W_C': w(ks[5], (INNER, STATE)), 'D': jnp.ones((INNER,), jnp.float32), 'W_out': w(ks[6], (INNER, HIDDEN))}
    _L0_attn_a_in = _L0_attn_a_setup()

    def _L0_attn_b_setup():
        import jax, jax.numpy as jnp
        import numpy as np
        D_MODEL = 128
        D_HEAD = 64
        key = jax.random.key(seed)
        k_x, k_q, k_k, k_v, k_o = jax.random.split(key, 5)
        scale = 1.0 / np.sqrt(D_MODEL)
        residual_stream = jax.random.normal(k_x, (4, 256, D_MODEL), dtype=jnp.float32)
        Q = scale * jax.random.normal(k_q, (D_MODEL, D_HEAD), dtype=jnp.float32)
        K = scale * jax.random.normal(k_k, (D_MODEL, D_HEAD), dtype=jnp.float32)
        V = scale * jax.random.normal(k_v, (D_MODEL, D_HEAD), dtype=jnp.float32)
        O = scale * jax.random.normal(k_o, (D_MODEL, D_HEAD), dtype=jnp.float32)
        return {'residual_stream': residual_stream, 'Q': Q, 'K': K, 'V': V, 'O': O}
    _L0_attn_b_in = _L0_attn_b_setup()

    def _L0_ffn_setup():
        import jax, jax.numpy as jnp
        import numpy as np
        DIM = 128
        DEPTH = 2
        HEADS = 8
        DIM_HEAD = 64
        WINDOW = 64
        INNER = HEADS * DIM_HEAD
        HID = int(DIM * 4 * 2 / 3)
        B, N = (2, 1024)
        QK_SCALE = 8.0

        def shift_token(t):
            t1, t2 = jnp.split(t, 2, axis=-1)
            t2 = jnp.pad(t2, ((0, 0), (1, 0), (0, 0)))[:, :-1]
            return jnp.concatenate([t1, t2], axis=-1)

        def l2norm(t):
            return t / jnp.clip(jnp.linalg.norm(t, axis=-1, keepdims=True), 1e-12)

        def rotate_half(x):
            x1, x2 = jnp.split(x, 2, axis=-1)
            return jnp.concatenate([-x2, x1], axis=-1)

        def rotary_xpos(q, k):
            n = q.shape[-2]
            half_idx = jnp.arange(0, DIM_HEAD, 2, dtype=jnp.float32)
            inv_freq = 1.0 / 10000.0 ** (half_idx / DIM_HEAD)
            t = jnp.arange(n, dtype=jnp.float32)
            freqs = t[:, None] * inv_freq[None, :]
            freqs = jnp.concatenate([freqs, freqs], axis=-1)
            base = (half_idx + 0.4 * DIM_HEAD) / (1.4 * DIM_HEAD)
            power = (t - n // 2) / float(WINDOW // 2)
            scale = base[None, :] ** power[:, None]
            scale = jnp.concatenate([scale, scale], axis=-1)
            cos, sin = (jnp.cos(freqs), jnp.sin(freqs))
            q = q * cos * scale + rotate_half(q) * sin * scale
            k = k * cos / scale + rotate_half(k) * sin / scale
            return (q, k)

        def local_attention(q, k, v):
            b, h, n, d = q.shape
            w = n // WINDOW
            bq = q.reshape(b, h, w, WINDOW, d) * QK_SCALE
            bk = k.reshape(b, h, w, WINDOW, d)
            bv = v.reshape(b, h, w, WINDOW, d)

            def look_around(t):
                p = jnp.pad(t, ((0, 0), (0, 0), (1, 0), (0, 0), (0, 0)))
                return jnp.concatenate([p[:, :, :w], p[:, :, 1:]], axis=3)
            bk, bv = (look_around(bk), look_around(bv))
            bt = jnp.arange(n).reshape(w, WINDOW)
            btp = jnp.pad(bt, ((1, 0), (0, 0)), constant_values=-1)
            btk = jnp.concatenate([btp[:w], btp[1:]], axis=1)
            sim = jnp.einsum('bhwid,bhwjd->bhwij', bq, bk)
            i = bt[:, :, None]
            j = btk[:, None, :]
            mask = (i < j) | (i > j + WINDOW) | (j == -1)
            sim = jnp.where(mask, -jnp.finfo(sim.dtype).max, sim)
            attn = jax.nn.softmax(sim, axis=-1)
            out = jnp.einsum('bhwij,bhwjd->bhwid', attn, bv)
            return out.reshape(b, h, n, d)

        def _layer(x, wqkv, qs, ksc, wo, lg, lb, w1, b1, w2, b2):
            b, n, _ = x.shape
            h = shift_token(x)
            qkv = h @ wqkv
            q, k, v = jnp.split(qkv, 3, axis=-1)
            to_heads = lambda t: t.reshape(b, n, HEADS, DIM_HEAD).transpose(0, 2, 1, 3)
            q, k, v = (to_heads(q), to_heads(k), to_heads(v))
            q = l2norm(q) * qs
            k = l2norm(k) * ksc
            q, k = rotary_xpos(q, k)
            o = local_attention(q, k, v)
            o = o.transpose(0, 2, 1, 3).reshape(b, n, INNER)
            x = x + o @ wo
            h = shift_token(x)
            mu = h.mean(-1, keepdims=True)
            var = h.var(-1, keepdims=True)
            h = (h - mu) / jnp.sqrt(var + 1e-05) * lg + lb
            h = h @ w1 + b1
            a, g = jnp.split(h, 2, axis=-1)
            h = a * jax.nn.gelu(g, approximate=False)
            x = x + h @ w2 + b2
            return x
        key = jax.random.key(seed)
        ks = jax.random.split(key, 6)
        return {'x': jax.random.normal(ks[0], (B, N, DIM), jnp.float32), 'wqkv': jax.random.normal(ks[1], (DEPTH, DIM, 3 * INNER), jnp.float32) * 0.02, 'q_scale': jnp.ones((DEPTH, DIM_HEAD), jnp.float32), 'k_scale': jnp.ones((DEPTH, DIM_HEAD), jnp.float32), 'wo': jax.random.normal(ks[2], (DEPTH, INNER, DIM), jnp.float32) * 0.02, 'ln_g': jnp.ones((DEPTH, DIM), jnp.float32), 'ln_b': jnp.zeros((DEPTH, DIM), jnp.float32), 'w1': jax.random.normal(ks[3], (DEPTH, DIM, 2 * HID), jnp.float32) * 0.02, 'b1': jnp.zeros((DEPTH, 2 * HID), jnp.float32), 'w2': jax.random.normal(ks[4], (DEPTH, HID, DIM), jnp.float32) * 0.02, 'b2': jnp.zeros((DEPTH, DIM), jnp.float32)}
    _L0_ffn_in = _L0_ffn_setup()

    def _L1_attn_a_setup():
        import jax, jax.numpy as jnp
        import numpy as np
        B, L, E, H = (2, 256, 128, 16)
        HD = E // H
        THETA = 10000.0

        def _rope_tables(seq_len, dim, dtype):
            inv_freq = 1.0 / THETA ** (jnp.arange(0, dim, 2, dtype=jnp.float32) / dim)
            freqs = jnp.arange(seq_len, dtype=jnp.float32)[:, None] * inv_freq[None, :]
            freqs = jnp.repeat(freqs, 2, axis=-1)
            return (jnp.cos(freqs).astype(dtype), jnp.sin(freqs).astype(dtype))

        def _rotate_half(x):
            x2 = x.reshape(*x.shape[:-1], -1, 2)
            x2 = jnp.stack([-x2[..., 1], x2[..., 0]], axis=-1)
            return x2.reshape(x.shape)

        def _apply_rope(x, cos, sin):
            return x * cos[None, None] + _rotate_half(x) * sin[None, None]
        key = jax.random.key(seed)
        ks = jax.random.split(key, 9)
        s = 1.0 / np.sqrt(E)
        return {'x': jax.random.normal(ks[0], (B, L, E), jnp.float32), 'Wq': jax.random.normal(ks[1], (E, E), jnp.float32) * s, 'bq': jax.random.normal(ks[2], (E,), jnp.float32) * 0.01, 'Wk': jax.random.normal(ks[3], (E, E), jnp.float32) * s, 'bk': jax.random.normal(ks[4], (E,), jnp.float32) * 0.01, 'Wv': jax.random.normal(ks[5], (E, E), jnp.float32) * s, 'bv': jax.random.normal(ks[6], (E,), jnp.float32) * 0.01, 'Wo': jax.random.normal(ks[7], (E, E), jnp.float32) * s, 'bo': jax.random.normal(ks[8], (E,), jnp.float32) * 0.01}
    _L1_attn_a_in = _L1_attn_a_setup()

    def _L1_attn_b_setup():
        import jax, jax.numpy as jnp
        import numpy as np
        B, T, C = (4, 256, 128)
        H, D = (16, 64)
        MAX_REL = 16
        NUM_BUCKETS = 2 * MAX_REL + 1
        key = jax.random.key(seed)
        ks = jax.random.split(key, 7)
        x = jax.random.normal(ks[0], (B, T, C), dtype=jnp.float32)
        Wq = jax.random.normal(ks[1], (H, C, D), dtype=jnp.float32) * 0.02
        Wk = jax.random.normal(ks[2], (H, C, D), dtype=jnp.float32) * 0.02
        Wv = jax.random.normal(ks[3], (H, C, D), dtype=jnp.float32) * 0.02
        Wp = jax.random.normal(ks[4], (H * D, C), dtype=jnp.float32) * 0.02
        bp = jnp.zeros((C,), dtype=jnp.float32)
        rel_table = jax.random.normal(ks[5], (NUM_BUCKETS, H), dtype=jnp.float32) * 0.02
        return {'x': x, 'Wq': Wq, 'Wk': Wk, 'Wv': Wv, 'Wp': Wp, 'bp': bp, 'rel_table': rel_table}
    _L1_attn_b_in = _L1_attn_b_setup()

    def _L1_ffn_setup():
        import jax, jax.numpy as jnp
        import numpy as np
        MAX_VAL = 100.0
        key = jax.random.key(seed)
        k1, k2, k3 = jax.random.split(key, 3)
        B, S, D_IN, D_OUT = (4, 1024, 128, 128)
        x = jax.random.normal(k1, (B, S, D_IN), dtype=jnp.float32)
        weights = jax.random.normal(k2, (D_OUT, D_IN), dtype=jnp.float32)
        scale = jnp.ones((D_OUT,), dtype=jnp.float32)
        bias = jax.random.normal(k3, (D_OUT,), dtype=jnp.float32)
        return {'x': x, 'weights': weights, 'scale': scale, 'bias': bias}
    _L1_ffn_in = _L1_ffn_setup()
    _d = {'L0_attn_a_x': _L0_attn_a_in['x'], 'L0_attn_a_W_in': _L0_attn_a_in['W_in'], 'L0_attn_a_conv_w': _L0_attn_a_in['conv_w'], 'L0_attn_a_conv_b': _L0_attn_a_in['conv_b'], 'L0_attn_a_W_dt': _L0_attn_a_in['W_dt'], 'L0_attn_a_b_dt': _L0_attn_a_in['b_dt'], 'L0_attn_a_W_B': _L0_attn_a_in['W_B'], 'L0_attn_a_W_C': _L0_attn_a_in['W_C'], 'L0_attn_a_D': _L0_attn_a_in['D'], 'L0_attn_a_W_out': _L0_attn_a_in['W_out'], 'L0_attn_b_Q': _L0_attn_b_in['Q'], 'L0_attn_b_K': _L0_attn_b_in['K'], 'L0_attn_b_V': _L0_attn_b_in['V'], 'L0_attn_b_O': _L0_attn_b_in['O'], 'L0_ffn_wqkv': _L0_ffn_in['wqkv'], 'L0_ffn_q_scale': _L0_ffn_in['q_scale'], 'L0_ffn_k_scale': _L0_ffn_in['k_scale'], 'L0_ffn_wo': _L0_ffn_in['wo'], 'L0_ffn_ln_g': _L0_ffn_in['ln_g'], 'L0_ffn_ln_b': _L0_ffn_in['ln_b'], 'L0_ffn_w1': _L0_ffn_in['w1'], 'L0_ffn_b1': _L0_ffn_in['b1'], 'L0_ffn_w2': _L0_ffn_in['w2'], 'L0_ffn_b2': _L0_ffn_in['b2'], 'L1_attn_a_Wq': _L1_attn_a_in['Wq'], 'L1_attn_a_bq': _L1_attn_a_in['bq'], 'L1_attn_a_Wk': _L1_attn_a_in['Wk'], 'L1_attn_a_bk': _L1_attn_a_in['bk'], 'L1_attn_a_Wv': _L1_attn_a_in['Wv'], 'L1_attn_a_bv': _L1_attn_a_in['bv'], 'L1_attn_a_Wo': _L1_attn_a_in['Wo'], 'L1_attn_a_bo': _L1_attn_a_in['bo'], 'L1_attn_b_Wq': _L1_attn_b_in['Wq'], 'L1_attn_b_Wk': _L1_attn_b_in['Wk'], 'L1_attn_b_Wv': _L1_attn_b_in['Wv'], 'L1_attn_b_Wp': _L1_attn_b_in['Wp'], 'L1_attn_b_bp': _L1_attn_b_in['bp'], 'L1_attn_b_rel_table': _L1_attn_b_in['rel_table'], 'L1_ffn_weights': _L1_ffn_in['weights'], 'L1_ffn_scale': _L1_ffn_in['scale'], 'L1_ffn_bias': _L1_ffn_in['bias']}
    _x0 = _d['L0_attn_a_x']
    _d['L0_attn_a_x'] = jax.random.normal(jax.random.fold_in(jax.random.key(seed), 1), (2, 1024, 128), dtype=_x0.dtype)
    del _x0
    return _d

def reference(L0_attn_a_x, L0_attn_a_W_in, L0_attn_a_conv_w, L0_attn_a_conv_b, L0_attn_a_W_dt, L0_attn_a_b_dt, L0_attn_a_W_B, L0_attn_a_W_C, L0_attn_a_D, L0_attn_a_W_out, L0_attn_b_Q, L0_attn_b_K, L0_attn_b_V, L0_attn_b_O, L0_ffn_wqkv, L0_ffn_q_scale, L0_ffn_k_scale, L0_ffn_wo, L0_ffn_ln_g, L0_ffn_ln_b, L0_ffn_w1, L0_ffn_b1, L0_ffn_w2, L0_ffn_b2, L1_attn_a_Wq, L1_attn_a_bq, L1_attn_a_Wk, L1_attn_a_bk, L1_attn_a_Wv, L1_attn_a_bv, L1_attn_a_Wo, L1_attn_a_bo, L1_attn_b_Wq, L1_attn_b_Wk, L1_attn_b_Wv, L1_attn_b_Wp, L1_attn_b_bp, L1_attn_b_rel_table, L1_ffn_weights, L1_ffn_scale, L1_ffn_bias):

    def _L0_attn_a_ref(x, W_in, conv_w, conv_b, W_dt, b_dt, W_B, W_C, D, W_out):
        import jax, jax.numpy as jnp
        import numpy as np
        HIDDEN = 128
        INNER = 256
        STATE = 64
        K = 4
        BATCH, SEQ = (2, 256)
        batch, seq_len, _ = x.shape
        inner = W_dt.shape[0]
        state_dim = W_B.shape[1]
        xz = x @ W_in
        x_inner, z = jnp.split(xz, 2, axis=-1)
        xc = jnp.transpose(x_inner, (0, 2, 1))
        k = conv_w.shape[-1]
        xc = jax.lax.conv_general_dilated(xc, conv_w, window_strides=(1,), padding=[(k - 1, 0)], dimension_numbers=('NCH', 'OIH', 'NCH'), feature_group_count=inner)
        xc = xc + conv_b[None, :, None]
        xc = jax.nn.silu(jnp.transpose(xc, (0, 2, 1)))
        dt = jax.nn.softplus(xc @ W_dt + b_dt)
        Bm = xc @ W_B
        Cm = xc @ W_C
        a = jnp.exp(-dt)
        dtx = dt * xc

        def step(state, inp):
            a_t, dtx_t, b_t, c_t = inp
            state = a_t[..., None] * state + dtx_t[..., None] * b_t[:, None, :]
            y_t = jnp.einsum('bin,bn->bi', state, c_t)
            return (state, y_t)
        init = jnp.zeros((batch, inner, state_dim), x.dtype)
        xs = (jnp.swapaxes(a, 0, 1), jnp.swapaxes(dtx, 0, 1), jnp.swapaxes(Bm, 0, 1), jnp.swapaxes(Cm, 0, 1))
        _, ys = jax.lax.scan(step, init, xs)
        y = jnp.swapaxes(ys, 0, 1) + D * xc
        y = y * jax.nn.silu(z)
        return y @ W_out

    def _L0_attn_b_ref(residual_stream, Q, K, V, O):
        import jax, jax.numpy as jnp
        import numpy as np
        D_MODEL = 128
        D_HEAD = 64
        queries = jnp.einsum('bsd,dh->bsh', residual_stream, Q)
        keys = jnp.einsum('bsd,dh->bsh', residual_stream, K)
        pre_attention = jnp.einsum('bqh,bkh->bqk', queries, keys)
        S = pre_attention.shape[-1]
        causal = jnp.tril(jnp.ones((S, S), dtype=bool))
        pre_attention = jnp.where(causal[None], pre_attention, -jnp.inf)
        attention = jax.nn.softmax(pre_attention, axis=-1)
        x = jnp.einsum('bsd,dh,eh->bse', residual_stream, V, O)
        return jnp.einsum('bqk,bke->bqe', attention, x)

    def _L0_ffn_ref(x, wqkv, q_scale, k_scale, wo, ln_g, ln_b, w1, b1, w2, b2):
        import jax, jax.numpy as jnp
        import numpy as np
        DIM = 128
        DEPTH = 2
        HEADS = 8
        DIM_HEAD = 64
        WINDOW = 64
        INNER = HEADS * DIM_HEAD
        HID = int(DIM * 4 * 2 / 3)
        B, N = (2, 1024)
        QK_SCALE = 8.0

        def shift_token(t):
            t1, t2 = jnp.split(t, 2, axis=-1)
            t2 = jnp.pad(t2, ((0, 0), (1, 0), (0, 0)))[:, :-1]
            return jnp.concatenate([t1, t2], axis=-1)

        def l2norm(t):
            return t / jnp.clip(jnp.linalg.norm(t, axis=-1, keepdims=True), 1e-12)

        def rotate_half(x):
            x1, x2 = jnp.split(x, 2, axis=-1)
            return jnp.concatenate([-x2, x1], axis=-1)

        def rotary_xpos(q, k):
            n = q.shape[-2]
            half_idx = jnp.arange(0, DIM_HEAD, 2, dtype=jnp.float32)
            inv_freq = 1.0 / 10000.0 ** (half_idx / DIM_HEAD)
            t = jnp.arange(n, dtype=jnp.float32)
            freqs = t[:, None] * inv_freq[None, :]
            freqs = jnp.concatenate([freqs, freqs], axis=-1)
            base = (half_idx + 0.4 * DIM_HEAD) / (1.4 * DIM_HEAD)
            power = (t - n // 2) / float(WINDOW // 2)
            scale = base[None, :] ** power[:, None]
            scale = jnp.concatenate([scale, scale], axis=-1)
            cos, sin = (jnp.cos(freqs), jnp.sin(freqs))
            q = q * cos * scale + rotate_half(q) * sin * scale
            k = k * cos / scale + rotate_half(k) * sin / scale
            return (q, k)

        def local_attention(q, k, v):
            b, h, n, d = q.shape
            w = n // WINDOW
            bq = q.reshape(b, h, w, WINDOW, d) * QK_SCALE
            bk = k.reshape(b, h, w, WINDOW, d)
            bv = v.reshape(b, h, w, WINDOW, d)

            def look_around(t):
                p = jnp.pad(t, ((0, 0), (0, 0), (1, 0), (0, 0), (0, 0)))
                return jnp.concatenate([p[:, :, :w], p[:, :, 1:]], axis=3)
            bk, bv = (look_around(bk), look_around(bv))
            bt = jnp.arange(n).reshape(w, WINDOW)
            btp = jnp.pad(bt, ((1, 0), (0, 0)), constant_values=-1)
            btk = jnp.concatenate([btp[:w], btp[1:]], axis=1)
            sim = jnp.einsum('bhwid,bhwjd->bhwij', bq, bk)
            i = bt[:, :, None]
            j = btk[:, None, :]
            mask = (i < j) | (i > j + WINDOW) | (j == -1)
            sim = jnp.where(mask, -jnp.finfo(sim.dtype).max, sim)
            attn = jax.nn.softmax(sim, axis=-1)
            out = jnp.einsum('bhwij,bhwjd->bhwid', attn, bv)
            return out.reshape(b, h, n, d)

        def _layer(x, wqkv, qs, ksc, wo, lg, lb, w1, b1, w2, b2):
            b, n, _ = x.shape
            h = shift_token(x)
            qkv = h @ wqkv
            q, k, v = jnp.split(qkv, 3, axis=-1)
            to_heads = lambda t: t.reshape(b, n, HEADS, DIM_HEAD).transpose(0, 2, 1, 3)
            q, k, v = (to_heads(q), to_heads(k), to_heads(v))
            q = l2norm(q) * qs
            k = l2norm(k) * ksc
            q, k = rotary_xpos(q, k)
            o = local_attention(q, k, v)
            o = o.transpose(0, 2, 1, 3).reshape(b, n, INNER)
            x = x + o @ wo
            h = shift_token(x)
            mu = h.mean(-1, keepdims=True)
            var = h.var(-1, keepdims=True)
            h = (h - mu) / jnp.sqrt(var + 1e-05) * lg + lb
            h = h @ w1 + b1
            a, g = jnp.split(h, 2, axis=-1)
            h = a * jax.nn.gelu(g, approximate=False)
            x = x + h @ w2 + b2
            return x
        for l in range(DEPTH):
            x = _layer(x, wqkv[l], q_scale[l], k_scale[l], wo[l], ln_g[l], ln_b[l], w1[l], b1[l], w2[l], b2[l])
        return x

    def _L1_attn_a_ref(x, Wq, bq, Wk, bk, Wv, bv, Wo, bo):
        import jax, jax.numpy as jnp
        import numpy as np
        B, L, E, H = (2, 256, 128, 16)
        HD = E // H
        THETA = 10000.0

        def _rope_tables(seq_len, dim, dtype):
            inv_freq = 1.0 / THETA ** (jnp.arange(0, dim, 2, dtype=jnp.float32) / dim)
            freqs = jnp.arange(seq_len, dtype=jnp.float32)[:, None] * inv_freq[None, :]
            freqs = jnp.repeat(freqs, 2, axis=-1)
            return (jnp.cos(freqs).astype(dtype), jnp.sin(freqs).astype(dtype))

        def _rotate_half(x):
            x2 = x.reshape(*x.shape[:-1], -1, 2)
            x2 = jnp.stack([-x2[..., 1], x2[..., 0]], axis=-1)
            return x2.reshape(x.shape)

        def _apply_rope(x, cos, sin):
            return x * cos[None, None] + _rotate_half(x) * sin[None, None]
        b, l, e = x.shape
        q = (x @ Wq.T + bq).reshape(b, l, H, HD).transpose(0, 2, 1, 3)
        k = (x @ Wk.T + bk).reshape(b, l, H, HD).transpose(0, 2, 1, 3)
        v = (x @ Wv.T + bv).reshape(b, l, H, HD).transpose(0, 2, 1, 3)
        cos, sin = _rope_tables(l, HD, x.dtype)
        q = _apply_rope(q, cos, sin)
        k = _apply_rope(k, cos, sin)
        scale = 1.0 / np.sqrt(HD)
        scores = jnp.einsum('bhsd,bhed->bhse', q, k) * scale
        attn = jax.nn.softmax(scores, axis=-1)
        out = jnp.einsum('bhse,bhed->bhsd', attn, v)
        out = out.transpose(0, 2, 1, 3).reshape(b, l, e)
        return out @ Wo.T + bo

    def _L1_attn_b_ref(x, Wq, Wk, Wv, Wp, bp, rel_table):
        import jax, jax.numpy as jnp
        import numpy as np
        B, T, C = (4, 256, 128)
        H, D = (16, 64)
        MAX_REL = 16
        NUM_BUCKETS = 2 * MAX_REL + 1
        Tq = x.shape[1]
        pos = jnp.arange(Tq)
        rel = pos[None, :] - pos[:, None]
        idx = jnp.clip(rel + MAX_REL, 0, NUM_BUCKETS - 1)
        bias = rel_table[idx]
        bias = jnp.transpose(bias, (2, 0, 1))
        q = jnp.einsum('btc,hcd->bhtd', x, Wq)
        k = jnp.einsum('btc,hcd->bhtd', x, Wk)
        v = jnp.einsum('btc,hcd->bhtd', x, Wv)
        scale = 1.0 / jnp.sqrt(jnp.float32(D))
        scores = jnp.einsum('bhtd,bhsd->bhts', q, k) * scale + bias[None]
        causal = jnp.tril(jnp.ones((Tq, Tq), dtype=bool))
        scores = jnp.where(causal[None, None], scores, jnp.float32(-jnp.inf))
        w = jax.nn.softmax(scores, axis=-1)
        out = jnp.einsum('bhts,bhsd->bhtd', w, v)
        out = jnp.transpose(out, (0, 2, 1, 3)).reshape(x.shape[0], Tq, H * D)
        return out @ Wp + bp

    def _L1_ffn_ref(x, weights, scale, bias):
        import jax, jax.numpy as jnp
        import numpy as np
        MAX_VAL = 100.0
        w = (weights >= 0.0).astype(x.dtype) * 2.0 - 1.0
        y = jnp.einsum('bsi,oi->bso', x, w)
        y = y * scale + bias
        y = jnp.clip(y, -MAX_VAL, MAX_VAL)
        return y
    x = L0_attn_a_x
    x = x + _L0_attn_a_ref(_layernorm(x, axis=-1), L0_attn_a_W_in, L0_attn_a_conv_w, L0_attn_a_conv_b, L0_attn_a_W_dt, L0_attn_a_b_dt, L0_attn_a_W_B, L0_attn_a_W_C, L0_attn_a_D, L0_attn_a_W_out)
    x = x + _L0_ffn_ref(_layernorm(x, axis=-1), L0_ffn_wqkv, L0_ffn_q_scale, L0_ffn_k_scale, L0_ffn_wo, L0_ffn_ln_g, L0_ffn_ln_b, L0_ffn_w1, L0_ffn_b1, L0_ffn_w2, L0_ffn_b2)
    x = x + _L0_attn_b_ref(_layernorm(x, axis=-1), L0_attn_b_Q, L0_attn_b_K, L0_attn_b_V, L0_attn_b_O)
    x = x + _L0_ffn_ref(_layernorm(x, axis=-1), L0_ffn_wqkv, L0_ffn_q_scale, L0_ffn_k_scale, L0_ffn_wo, L0_ffn_ln_g, L0_ffn_ln_b, L0_ffn_w1, L0_ffn_b1, L0_ffn_w2, L0_ffn_b2)
    x = x + _L1_attn_a_ref(_layernorm(x, axis=-1), L1_attn_a_Wq, L1_attn_a_bq, L1_attn_a_Wk, L1_attn_a_bk, L1_attn_a_Wv, L1_attn_a_bv, L1_attn_a_Wo, L1_attn_a_bo)
    x = x + _L1_ffn_ref(_layernorm(x, axis=-1), L1_ffn_weights, L1_ffn_scale, L1_ffn_bias)
    x = x + _L1_attn_b_ref(_layernorm(x, axis=-1), L1_attn_b_Wq, L1_attn_b_Wk, L1_attn_b_Wv, L1_attn_b_Wp, L1_attn_b_bp, L1_attn_b_rel_table)
    x = x + _L1_ffn_ref(_layernorm(x, axis=-1), L1_ffn_weights, L1_ffn_scale, L1_ffn_bias)
    return x

_drawn_inputs = setup_inputs


def setup_inputs(seed=0):
    import zlib

    import numpy as np

    out = dict(_drawn_inputs(seed))
    spreads = {'L0_attn_a_conv_b': (0.0, 0.1),
     'L0_attn_a_D': (1.0, 0.2),
     'L0_ffn_q_scale': (1.0, 0.2),
     'L0_ffn_k_scale': (1.0, 0.2),
     'L0_ffn_ln_g': (1.0, 0.2),
     'L0_ffn_ln_b': (0.0, 0.1),
     'L0_ffn_b1': (0.0, 0.1),
     'L0_ffn_b2': (0.0, 0.1),
     'L1_attn_b_bp': (0.0, 0.1),
     'L1_ffn_scale': (1.0, 0.2)}
    factors = {}
    for name, (base, spread) in spreads.items():
        noise = np.random.default_rng([zlib.crc32(name.encode()), seed]).standard_normal(out[name].shape)
        drawn = base * np.exp(spread * noise) if base else spread * noise
        out[name] = jnp.asarray(drawn.astype(out[name].dtype))
    for name, factor in factors.items():
        out[name] = (out[name] * factor).astype(out[name].dtype)
    return out
```

```python
from contextlib import ExitStack

import numpy as np

import concourse.bass as bass
from concourse import mybir
from concourse.alu_op_type import AluOpType as ALU

ACT = mybir.ActivationFunctionType
F32 = mybir.dt.float32
BF16 = mybir.dt.bfloat16
AX_X = mybir.AxisListType.X
ds = bass.ds

P = 128
B, S = 2, 1024
GW = 512
NG = B * S // GW
GB = S // GW
NT = B * S // P
TB = S // P
EPS = 1e-5
LN_EXP = "natural_log_exp_and_others"

INNER, STATE, TAPS = 256, 64, 4
HALVES = INNER // P
DBC = INNER + 2 * STATE
WM_DBC = 2 * HALVES * P
WM_OUT = WM_DBC + HALVES * DBC
WM_V = WM_OUT + HALVES * P
WM_N = WM_V + HALVES * 6
LEVELS = [64, 32, 16, 8, 4, 2, 1]
NL = len(LEVELS)
Q_IN, Q_END, Q_ALL = NL, NL + 1, NL + 2

DEPTH, HEADS, DH, WINDOW = 2, 8, 64, 64
CH = HEADS // 2
HID = 341
HC = 3
BAND = P + WINDOW
WL_Q, WL_O, WL_1, WL_2 = 0, 5 * CH * P, 5 * CH * P + CH * P, 5 * CH * P + CH * P + 2 * HC * P
WL_V = WL_2 + HC * P
V_QK, V_B1, V_G, V_B, V_B2 = 0, 4, 10, 11, 12
WL_N = WL_V + 13
RH, RD = 16, 8

REL = 16
NEAR = P + REL
MAX_VAL = 100.0
STAGE_BASE = 51 * 1024
SBUF_END = 229344
NORM_SCALE = 2.0 ** 30


class Gate:

    def __init__(self):
        self.n = 0


def build(nc, ins, out, last=99):
    ctx = ExitStack()
    with ctx:
        def scope(*specs):
            at, out_ = STAGE_BASE, []
            for name, shape, *dt in specs:
                dt = dt[0] if dt else F32
                out_.append(nc.alloc_sbuf_tensor_at(name, shape, dt, offset=at))
                at += -(-int(np.prod(shape[1:])) * mybir.dt.size(dt) // 64) * 64
            assert at <= SBUF_END, (specs[0][0], at)
            return out_

        def sb(name, shape, dt=F32):
            return ctx.enter_context(nc.sbuf_tensor(name, shape, dt))

        def sem(name):
            return ctx.enter_context(nc.semaphore(name))

        ps = ctx.enter_context(nc.psum_tensor("ps", [P, 8, GW], F32))
        bank = [ps[:, i, :] for i in range(8)]
        parts = nc.dram_tensor("parts", (6, B * P, S), BF16, kind="Internal").ap()
        bias_rows = nc.dram_tensor("bias_rows", (16, P + NEAR), F32, kind="Internal").ap()

        xT = sb("xT", [P, B, S])
        nT = sb("nT", [P, B, S])
        ident = sb("ident", [P, P])
        identb = sb("identb", [P, P], BF16)
        meanw = sb("meanw", [P, P])
        headw = sb("headw", [P, P])
        lnx = sb("lnx", [P, NG, GW])
        lns = sb("lns", [P, NG, GW])
        cols = sb("cols", [P, 4])

        stage_done = sem("stage_done")
        stored = sem("stored")
        gates = {}

        def gate(eng, extra=0):
            g = gates.setdefault(eng.engine, Gate())
            g.n += 1
            eng.drain().then_inc(stage_done, 1)
            eng.wait_ge(stage_done, 4 * g.n)

        def group(t, g):
            return t[:, g // GB, (g % GB) * GW:(g % GB + 1) * GW]

        class Layernorm:
            def __init__(self, name, src, dst):
                self.src, self.dst, self.xc, self.sq = src, dst, lnx, lns
                self.mean_ready = sem(name + "_mean_ready")
                self.centred = sem(name + "_centred")
                self.sq_ready = sem(name + "_sq_ready")
                self.var_ready = sem(name + "_var_ready")
                self.ln_done = sem(name + "_ln_done")
                self.rstd_ready = sem(name + "_rstd_ready")
                self.normed = sem(name + "_normed")

            def pe(self, pe, n=0):
                for g in range(NG):
                    pe.matmul(bank[g][:, :], meanw[:, :], group(self.src, g), start=True, stop=True)\
                        .then_inc(self.mean_ready, 1)
                for g in range(NG):
                    pe.wait_ge(self.sq_ready, NG * n + g + 1)
                    pe.matmul(bank[4 + g][:, :], meanw[:, :], self.sq[:, g, :], start=True, stop=True)\
                        .then_inc(self.var_ready, 1)

            def dve(self, v, n=0, gain=None, shift=None):
                for g in range(NG):
                    v.wait_ge(self.mean_ready, NG * n + g + 1)
                    v.tensor_tensor(self.xc[:, g, :], group(self.src, g), bank[g][:, :], ALU.subtract)\
                        .then_inc(self.centred, 1)
                for g in range(NG):
                    v.wait_ge(self.rstd_ready, NG * n + g + 1)
                    if gain is None:
                        v.tensor_tensor(group(self.dst, g), self.xc[:, g, :], self.sq[:, g, :], ALU.mult)\
                            .then_inc(self.normed, 1)
                    else:
                        v.scalar_tensor_tensor(group(self.dst, g), self.xc[:, g, :], gain,
                                               self.sq[:, g, :], ALU.mult, ALU.mult).then_inc(self.normed, 1)
                        v.wait_ge(self.normed, 2 * (NG * n + g) + 1)
                        v.tensor_scalar(group(self.dst, g), group(self.dst, g), shift, None, ALU.add)\
                            .then_inc(self.normed, 1)

            def act(self, a, n=0):
                for g in range(NG):
                    a.wait_ge(self.centred, NG * n + g + 1)
                    a.activation(self.sq[:, g, :], self.xc[:, g, :], ACT.Square).then_inc(self.sq_ready, 1)
                for g in range(NG):
                    a.wait_ge(self.var_ready, NG * n + g + 1)
                    a.activation(self.sq[:, g, :], bank[4 + g][:, :], ACT.Ln, bias=cols[:, 0:1])\
                        .then_inc(self.ln_done, 1)
                    a.wait_ge(self.ln_done, NG * n + g + 1)
                    a.activation(self.sq[:, g, :], self.sq[:, g, :], ACT.Exp, scale=-0.5)\
                        .then_inc(self.rstd_ready, 1)

        ln_x = Layernorm("ln", xT, nT)
        LN_CALLS = {"mamba": 0, "t1": 1, "ca": 2, "t2": 3, "ra": 4, "s1": 5, "cm": 6, "s2": 7}

        xin, = scope(("xin", [P, NT, P]))
        in_loaded, const_loaded = sem("in_loaded"), sem("const_loaded")
        xpose_ready = sem("xpose_ready")

        def load_sp(sp):
            sp.dma_start(ident[:, :], ins["ident"]).then_inc(const_loaded, 16)
            sp.dma_start(xin[:, :, :], ins["x"].rearrange("b (t p) f -> p (b t) f", p=P)).then_inc(in_loaded, 16)
            sp.dma_start(identb[:, :], ins["identb"]).then_inc(const_loaded, 16)
            sp.dma_start(meanw[:, :], ins["meanw"]).then_inc(const_loaded, 16)
            sp.dma_start(headw[:, :], ins["headw"]).then_inc(const_loaded, 16)

        def load_pe(pe):
            pe.wait_ge(const_loaded, 64)
            pe.wait_ge(in_loaded, 16)
            for t in range(NT):
                mm = pe.transpose(bank[t // 4][:, (t % 4) * P:(t % 4 + 1) * P], xin[:, t, :], ident[:, :])
                if t % 4 == 3:
                    mm.then_inc(xpose_ready, 1)

        def load_dve(v):
            for g in range(NG):
                v.wait_ge(xpose_ready, g + 1)
                v.tensor_copy(group(xT, g), bank[g][:, :])

        def load_act(a):
            a.preload_act_table_set(LN_EXP)

        def load_pool(p):
            p.memset(cols[:, 0:1], EPS)
            p.memset(cols[:, 1:2], 2.0 ** -60)
            p.memset(cols[:, 3:4], 0.0)
            p.memset(cols[:, 2:3], 15.0 * float(np.log(2.0)))

        (zs, xi, xc, wm, qmat, gmask, bdt, xct, uu, ee, dtt, dtx, bcs, bct, gm, ev, xv, tv, hst, ya) = scope(
            ("zs", [P, HALVES, B, S]), ("xi", [P, HALVES, B, S + TAPS - 1]), ("xc", [P, HALVES, B, S]),
            ("wm", [P, WM_N]), ("qmat", [P, NL + 3, P]), ("gmask", [P, NL + 1, P]), ("bdt", [P, INNER]),
            ("xct", [P, HALVES, B, P]), ("uu", [P, B, INNER]), ("ee", [P, B, INNER]),
            ("dtt", [P, B, INNER]), ("dtx", [P, B, INNER]), ("bcs", [P, B, P]), ("bct", [P, 2 * B, P]),
            ("gm", [P, B, NL + 1, P]), ("ev", [P, 3, B, INNER]), ("xv", [P, 3, B, INNER]),
            ("tv", [P, 3, B, INNER]), ("hst", [P, B, INNER]), ("ya", [P, B, INNER]))
        w_in = wm[:, 0:WM_DBC].rearrange("p (c n) -> p c n", c=4)
        w_dbc = wm[:, WM_DBC:WM_OUT].rearrange("p (h n) -> p h n", h=HALVES)
        w_out = wm[:, WM_OUT:WM_V].rearrange("p (h n) -> p h n", h=HALVES)
        conv_v = wm[:, WM_V:WM_N].rearrange("p (h n) -> p h n", h=HALVES)
        (mw_loaded, pads_set, in_ready, x_copied, z_copied, conv_done, silu_done, xct_ready, dbc_ready,
         u_ready, sp_done, bcs_ready, dt_ready, dtx_ready, bct_psum, bct_ready, g_psum, gm_ready,
         q_ready, e_ready, x_ready, y_ready, y_used, acc_done, h_done, yt_ready, out_done, mo_ready) = [
            sem("m_" + n) for n in (
                "mw_loaded pads_set in_ready x_copied z_copied conv_done silu_done xct_ready dbc_ready "
                "u_ready sp_done bcs_ready dt_ready dtx_ready bct_psum bct_ready g_psum gm_ready "
                "q_ready e_ready x_ready y_ready y_used acc_done h_done yt_ready out_done mo_ready "
                "").split()]
        QSTEPS = [Q_IN] + list(range(NL)) + [Q_END, Q_ALL]
        NQ = len(QSTEPS)
        NX = NL + 1
        NY = NL + 3

        class Mamba:
            def sp(self, sp):
                for dst, src in ((wm[:, :], ins["wm"]), (qmat[:, :, :], ins["qmat"]), (gmask[:, :, :], ins["gmask"]),
                                 (bdt[:, :], ins["b_dt"].partition_broadcast(P))):
                    sp.dma_start(dst, src).then_inc(mw_loaded, 16)

            def pe(self, pe):
                ln_x.pe(pe, LN_CALLS["mamba"])
                pe.wait_ge(mw_loaded, 64)
                for g in range(NG):
                    pe.wait_ge(ln_x.normed, NG if g else 1)
                    if g >= 2:
                        pe.wait_ge(x_copied, 2 * (g - 1))
                        pe.wait_ge(z_copied, 2 * (g - 1))
                    for c in range(4):
                        mm = pe.matmul(bank[4 * (g % 2) + c][:, :], w_in[:, c, :], group(nT, g), start=True, stop=True)
                    mm.then_inc(in_ready, 1)
                pe.wait_ge(x_copied, 2 * NG)
                pe.wait_ge(z_copied, 2 * NG)
                pe.wait_ge(pads_set, 3)
                with pe.Fori(0, TB) as c:
                    pe.wait_ge(xct_ready, HALVES * (c + 1))
                    pe.wait_ge(y_used, (NY - 1) * c)
                    for b in range(B):
                        for h in range(HALVES):
                            k = b * HALVES + h
                            pe.transpose(bank[2][:, k * P:(k + 1) * P], xct[:, h, b, :], ident[:, :])
                    pe.wait_ge(h_done, 2 * c)
                    for b in range(B):
                        for h in range(HALVES):
                            mm = pe.matmul(bank[b][:, 0:DBC], xct[:, h, b, :], w_dbc[:, h, :], start=h == 0, stop=h == HALVES - 1)
                    mm.then_inc(dbc_ready, 1)
                    pe.wait_ge(bcs_ready, 2 * c + 2)
                    pe.wait_ge(out_done, 4 * c)
                    for b in range(B):
                        mm = pe.transpose(bank[3][:, b * P:(b + 1) * P], bcs[:, b, :], ident[:, :])
                    mm.then_inc(bct_psum, 1)
                    pe.wait_ge(bct_ready, 2 * c + 2)
                    for b in range(B):
                        mm = pe.matmul(bank[4][:, b * P:(b + 1) * P], bct[:, b, :], bct[:, B + b, :], start=True, stop=True)
                    mm.then_inc(g_psum, 1)
                    pe.wait_ge(dt_ready, c + 1)

                    def decay(j):
                        pe.wait_ge(e_ready, NQ * c + max(j - 2, 0))
                        pe.matmul(bank[5 + j % 3][:, :], qmat[:, QSTEPS[j], :], dtt[:, :, :], start=True, stop=True)\
                            .then_inc(q_ready, 1)

                    for j in range(3):
                        decay(j)
                    for i in range(NY):
                        if i >= 3:
                            pe.wait_ge(y_used, (NY - 1) * c + i - 2)
                        if i == 0:
                            pe.wait_ge(gm_ready, 2 * c + 2)
                            pe.wait_ge(dtx_ready, c + 1)
                        elif i == 1:
                            pe.wait_ge(h_done, 2 * c)
                        else:
                            pe.wait_ge(x_ready, NX * c + i - 1)
                        for b in range(B):
                            o, start = bank[i % 3][:, b * INNER:(b + 1) * INNER], True
                            if i == 0:
                                mm = pe.matmul(o, gm[:, b, NL, :], dtx[:, b, :], start=True, stop=True)
                            elif i == 1:
                                mm = pe.matmul(o, bct[:, B + b, :], hst[:, b, :], start=True, stop=True)
                            elif i < NY - 1:
                                mm = pe.matmul(o, gm[:, b, i - 2, :], xv[:, (i - 2) % 3, b, :], start=True, stop=True)
                            else:
                                mm = pe.matmul(bank[i % 3][0:STATE, b * INNER:(b + 1) * INNER], bcs[:, b, 0:STATE],
                                               xv[:, (i - 2) % 3, b, :], start=True, stop=True)
                        mm.then_inc(y_ready, 1)
                        if i + 3 < NQ:
                            decay(i + 3)
                    pe.wait_ge(acc_done, (NY - 2) * (c + 1))
                    for k in range(HALVES * B):
                        mm = pe.transpose(bank[3][:, k * P:(k + 1) * P],
                                          ya[:, k % B, (k // B) * P:(k // B + 1) * P], ident[:, :])
                    mm.then_inc(yt_ready, 1)
                pe.wait_ge(out_done, 4 * TB)
                pe.wait_ge(h_done, 2 * TB)
                for g in range(NG):
                    for h in range(HALVES):
                        mm = pe.matmul(bank[g][:, :], w_out[:, h, :], group(zs[:, h, :, :], g),
                                       start=h == 0, stop=h == HALVES - 1)
                    mm.then_inc(mo_ready, 1)

            def act(self, a):
                ln_x.act(a, LN_CALLS["mamba"])
                for g in range(NG):
                    a.wait_ge(in_ready, g + 1)
                    for h in range(HALVES):
                        b, t0 = g // GB, (g % GB) * GW + TAPS - 1
                        a.activation(xi[:, h, b, t0:t0 + GW], bank[4 * (g % 2) + h][:, :], ACT.Copy).then_inc(x_copied, 1)
                a.wait_ge(z_copied, 2 * NG)
                a.activation(zs[:, :, :, :], zs[:, :, :, :], ACT.Silu).then_inc(silu_done, 1)
                for h in range(HALVES):
                    a.wait_ge(conv_done, TAPS * (h + 1))
                    a.activation(xc[:, h, :, :], xc[:, h, :, :], ACT.Silu).then_inc(silu_done, 1)
                a.preload_act_table_set(LN_EXP)
                with a.Fori(0, TB) as c:
                    for b in range(B):
                        a.wait_ge(u_ready, 2 * c + b + 1)
                        a.activation(bcs[:, b, :], bank[b][:, INNER:DBC], ACT.Copy).then_inc(bcs_ready, 1)
                    a.wait_ge(u_ready, 2 * c + 2)
                    a.activation(ee[:, :, :], uu[:, :, :], ACT.Abs).then_inc(sp_done, 1)
                    a.wait_ge(sp_done, 3 * c + 1)
                    a.activation(ee[:, :, :], ee[:, :, :], ACT.Exp, scale=-1.0).then_inc(sp_done, 1)
                    a.wait_ge(sp_done, 3 * c + 2)
                    a.activation(ee[:, :, :], ee[:, :, :], ACT.Ln, bias=1.0).then_inc(sp_done, 1)
                    for j in range(NQ):
                        if j < 3:
                            a.wait_ge(h_done, 2 * c)
                        else:
                            a.wait_ge(y_used, (NY - 1) * c + j - 1)
                        a.wait_ge(q_ready, NQ * c + j + 1)
                        a.activation(ev[:, j % 3, :, :], bank[5 + j % 3][:, :], ACT.Exp, scale=-1.0).then_inc(e_ready, 1)

            def pool(self, p):
                p.memset(xi[:, :, :, 0:TAPS - 1], 0.0).then_inc(pads_set, 1)
                p.memset(bct[:, :, :], 0.0).then_inc(pads_set, 1)
                p.memset(hst[:, :, :], 0.0).then_inc(pads_set, 1)
                p.wait_ge(silu_done, 1 + HALVES)
                with p.Fori(0, TB) as c:
                    p.wait_ge(dbc_ready, c)
                    for h in range(HALVES):
                        p.tensor_copy(xct[:, h, :, :], xc[:, h, :, ds(c * P, P)]).then_inc(xct_ready, 1)
                    p.wait_ge(dtx_ready, c + 1)
                    for k in range(NX):
                        p.wait_ge(e_ready, NQ * c + k + 2)
                        p.wait_ge(y_ready, NY * c + (k if k >= 3 else 0))
                        p.tensor_tensor(xv[:, k % 3, :, :], ev[:, (k + 1) % 3, :, :], dtx[:, :, :], ALU.mult)\
                            .then_inc(x_ready, 1)

            def dve(self, v):
                ln_x.dve(v, LN_CALLS["mamba"])
                for g in range(NG):
                    v.wait_ge(in_ready, g + 1)
                    for h in range(HALVES):
                        v.tensor_copy(group(zs[:, h, :, :], g), bank[4 * (g % 2) + HALVES + h][:, :]).then_inc(z_copied, 1)
                v.wait_ge(x_copied, 2 * NG)
                v.wait_ge(pads_set, 3)
                v.wait_ge(mw_loaded, 64)
                for h in range(HALVES):
                    v.tensor_scalar(xc[:, h, :, :], xi[:, h, :, 0:S], conv_v[:, h, 0:1], conv_v[:, h, 4:5],
                                    ALU.mult, ALU.add).then_inc(conv_done, 1)
                    for k in range(1, TAPS):
                        v.wait_ge(conv_done, TAPS * h + k)
                        v.scalar_tensor_tensor(xc[:, h, :, :], xi[:, h, :, k:k + S], conv_v[:, h, k:k + 1],
                                               xc[:, h, :, :], ALU.mult, ALU.add).then_inc(conv_done, 1)
                with v.Fori(0, TB) as c:
                    v.wait_ge(dbc_ready, c + 1)
                    for b in range(B):
                        v.tensor_tensor(uu[:, b, :], bank[b][:, 0:INNER], bdt[:, :], ALU.add).then_inc(u_ready, 1)
                    v.wait_ge(y_ready, NY * c)
                    v.wait_ge(bct_psum, c + 1)
                    for k in range(2):
                        v.tensor_copy(bct[0:STATE, k * B:(k + 1) * B, :], bank[3][k * STATE:(k + 1) * STATE, 0:B * P]
                                      .rearrange("p (b s) -> p b s", b=B)).then_inc(bct_ready, 1)
                    v.wait_ge(sp_done, 3 * c + 3)
                    v.wait_ge(q_ready, NQ * c)
                    v.scalar_tensor_tensor(dtt[:, :, :], uu[:, :, :], 0.0, ee[:, :, :], ALU.max, ALU.add)\
                        .then_inc(dt_ready, 1)
                    v.wait_ge(dt_ready, c + 1)
                    v.wait_ge(x_ready, NX * c)
                    v.tensor_tensor(dtx[:, :, :], dtt[:, :, :], bank[2][:, :].rearrange("p (b i) -> p b i", b=B),
                                    ALU.mult).then_inc(dtx_ready, 1)
                    v.wait_ge(g_psum, c + 1)
                    for b in range(B):
                        v.tensor_tensor(gm[:, b, :, :], gmask[:, :, :],
                                        bank[4][:, b * P:(b + 1) * P].unsqueeze(1).broadcast_to([P, NL + 1, P]),
                                        ALU.mult).then_inc(gm_ready, 1)
                    v.wait_ge(y_ready, NY * c + 1)
                    v.wait_ge(yt_ready, c)
                    v.tensor_copy(ya[:, :, :], bank[0][:, :].rearrange("p (b i) -> p b i", b=B)).then_inc(y_used, 1)
                    for i in range(1, NY - 1):
                        v.wait_ge(y_ready, NY * c + i + 1)
                        v.wait_ge(e_ready, NQ * c + i)
                        if i == 1:
                            v.wait_ge(y_used, (NY - 1) * c + 1)
                        v.tensor_tensor(tv[:, i % 3, :, :], ev[:, (i - 1) % 3, :, :],
                                        bank[i % 3][:, :].rearrange("p (b i) -> p b i", b=B), ALU.mult).then_inc(y_used, 1)
                        v.wait_ge(y_used, (NY - 1) * c + i + 1)
                        v.wait_ge(acc_done, (NY - 2) * c + i - 1)
                        v.tensor_tensor(ya[:, :, :], ya[:, :, :], tv[:, i % 3, :, :], ALU.add).then_inc(acc_done, 1)
                    v.wait_ge(e_ready, NQ * c + NQ)
                    v.tensor_tensor(hst[0:STATE, :, :], hst[0:STATE, :, :], ev[0:STATE, (NQ - 1) % 3, :, :], ALU.mult)\
                        .then_inc(h_done, 1)
                    v.wait_ge(h_done, 2 * c + 1)
                    v.wait_ge(y_ready, NY * c + NY)
                    v.tensor_tensor(hst[0:STATE, :, :], hst[0:STATE, :, :],
                                    bank[(NY - 1) % 3][0:STATE, :].rearrange("p (b i) -> p b i", b=B), ALU.add)\
                        .then_inc(h_done, 1)
                    v.wait_ge(h_done, 2 * c + 2)
                    v.wait_ge(yt_ready, c + 1)
                    for h in range(HALVES):
                        v.scalar_tensor_tensor(tv[:, h, :, 0:P], xc[:, h, :, ds(c * P, P)], conv_v[:, h, 5:6],
                                               bank[3][:, h * B * P:(h + 1) * B * P].rearrange("p (b t) -> p b t", b=B),
                                               ALU.mult, ALU.add).then_inc(out_done, 1)
                        v.wait_ge(out_done, 4 * c + 2 * h + 1)
                        v.tensor_tensor(zs[:, h, :, ds(c * P, P)], zs[:, h, :, ds(c * P, P)], tv[:, h, :, 0:P], ALU.mult)\
                            .then_inc(out_done, 1)
                for g in range(NG):
                    v.wait_ge(mo_ready, g + 1)
                    v.tensor_tensor(group(xT, g), group(xT, g), bank[g][:, :], ALU.add)

        mamba = Mamba()

        (rot, wl, wc, hT, vc, qm, kk, oT, pt, rd, ab, cq, rv, gl, uh, maskb) = scope(
            ("rot", [P, 4, S]), ("wl", [P, WL_N]), ("wc", [P, 5, P]), ("hT", [P, B, S + 1]),
            ("vc", [P, NT, 2, P]), ("qm", [P, 2, B * S]), ("kk", [P, B, S]), ("oT", [P, CH, B * S]),
            ("pt", [P, 3, 2, BAND]), ("rd", [P, 2, GW]), ("ab", [P, 2, 4, GW]), ("cq", [P, 2, 2, GW]),
            ("rv", [P, 2, 2, GW]), ("gl", [P, HC, GW]), ("uh", [P, HC, GW]), ("maskb", [P, 2, BAND], BF16))
        wl_qkv = wl[:, WL_Q:WL_O].rearrange("p (k cn) -> p k cn", k=5)
        wl_o = wl[:, WL_O:WL_1].rearrange("p (c n) -> p c n", c=CH)
        wl_1 = wl[:, WL_1:WL_2].rearrange("p (c n) -> p c n", c=2 * HC)
        wl_2 = wl[:, WL_2:WL_V].rearrange("p (c n) -> p c n", c=HC)
        vec = wl[:, WL_V:WL_N]

        def keys_of(t):
            return P if t % TB == TB - 1 else BAND

        class Transformer:
            def __init__(self, name):
                self.ln1 = Layernorm(name + "_ln1", hT[:, :, 0:S], kk)
                self.tab_loaded = sem(name + "_tab_loaded")
                self.wq_loaded = sem(name + "_wq_loaded")
                self.wl_loaded = sem(name + "_wl_loaded")
                self.preset = sem(name + "_preset")
                self.shifted = sem(name + "_shifted")
                self.wc_ready = sem(name + "_wc_ready")
                self.proj_ready = sem(name + "_proj_ready")
                self.sq_ready = sem(name + "_sq_ready")
                self.ab_done = sem(name + "_ab_done")
                self.add_done = sem(name + "_add_done")
                self.norm_ready = sem(name + "_norm_ready")
                self.nln_done = sem(name + "_nln_done")
                self.rinv_ready = sem(name + "_rinv_ready")
                self.qk_done = sem(name + "_qk_done")
                self.v_ready = sem(name + "_v_ready")
                self.v_copied = sem(name + "_v_copied")
                self.sim_ready = sem(name + "_sim_ready")
                self.exp_done = sem(name + "_exp_done")
                self.pv_ready = sem(name + "_pv_ready")
                self.rd_done = sem(name + "_rd_done")
                self.o_done = sem(name + "_o_done")
                self.wo_ready = sem(name + "_wo_ready")
                self.wo_added = sem(name + "_wo_added")
                self.hid_ready = sem(name + "_hid_ready")
                self.gelu_done = sem(name + "_gelu_done")
                self.u_done = sem(name + "_u_done")
                self.out_ready = sem(name + "_out_ready")
                self.out_added = sem(name + "_out_added")

            def sp(self, sp, g0, k):
                sp.dma_start(rot[:, :, :], ins["rot"]).then_inc(self.tab_loaded, 16)
                sp.dma_start(maskb[:, :, :], ins["maskb"]).then_inc(self.tab_loaded, 16)

                def load(l, c0, c1, done):
                    sp.dma_start(wl[:, c0:c1], ins["wl"][ds(l - k * DEPTH, 1), :, c0:c1].rearrange("a p n -> (a p) n"))\
                        .then_inc(done, 16)

                def rest(l):
                    sp.wait_ge(stage_done, 4 * l + 4 * (g0 - k * DEPTH))
                    load(l, WL_V, WL_N, self.wq_loaded)
                    load(l, WL_O, WL_V, self.wl_loaded)

                load(k * DEPTH, WL_Q, WL_O, self.wq_loaded)
                with sp.Fori(k * DEPTH, (k + 1) * DEPTH - 1) as l:
                    rest(l)
                    sp.wait_ge(self.wc_ready, CH * (l + 1))
                    load(l + 1, WL_Q, WL_O, self.wq_loaded)
                rest((k + 1) * DEPTH - 1)

            def pool(self, p, k):
                p.memset(qm[DH:P, 0, :], 0.0).then_inc(self.preset, 1)
                p.memset(qm[0:DH, 1, :], 0.0).then_inc(self.preset, 1)
                p.wait_ge(self.preset, 5 * k + 2)
                p.memset(vc[:, :, :, :], 1.0).then_inc(self.preset, 1)
                p.wait_ge(self.preset, 5 * k + 3)
                for b in range(B):
                    p.memset(hT[DH:P, b, 0:1], 0.0).then_inc(self.preset, 1)
                p.wait_ge(self.preset, 5 * k + 5)
                with p.Fori(k * DEPTH, (k + 1) * DEPTH) as l:
                    with p.Fori(0, CH) as c:
                        n = l * CH + c
                        p.wait_ge(self.wq_loaded, 32 * l + 32)
                        p.wait_ge(self.v_ready, 4 * n)
                        p.tensor_copy(wc[:, :, :], wl_qkv[:, :, ds(c * P, P)]).then_inc(self.wc_ready, 1)
                        for g in range(NG):
                            p.wait_ge(self.qk_done, 12 * n + (3 * (g - 1) if g >= 2 else 0))
                            for qk in range(2):
                                p.wait_ge(self.ab_done, 16 * n + 4 * g + 2 * qk + 2)
                                p.tensor_tensor(cq[:, g % 2, qk, :], ab[:, g % 2, 2 * qk, :], ab[:, g % 2, 2 * qk + 1, :],
                                                ALU.add).then_inc(self.add_done, 1)
                    layer_gate(p, l - k * DEPTH)
                end_layers(p)

            def pe(self, pe, k):
                ln_x.pe(pe, 1 + 2 * k)
                pe.wait_ge(self.preset, 5 * k + 5)
                pe.wait_ge(self.tab_loaded, 32 * k + 32)
                with pe.Fori(k * DEPTH, (k + 1) * DEPTH) as l:
                    with pe.Fori(0, CH) as c:
                        n = l * CH + c
                        pe.wait_ge(self.shifted, 4 * l + 2)
                        pe.wait_ge(self.wc_ready, n + 1)

                        def project(g):
                            if g == 0:
                                pe.wait_ge(self.exp_done, 16 * n)
                            for j, (w, bk) in enumerate(((1, 1), (0, 0), (3, 3), (2, 2))):
                                if g == 0 and j == 2:
                                    pe.wait_ge(self.o_done, 8 * n)
                                if g > 0:
                                    pe.wait_ge(self.ab_done, 16 * n + 4 * (g - 1) + j + 1)
                                pe.matmul(bank[bk][:, :], wc[:, w, :], group(hT, g), start=True, stop=True)\
                                    .then_inc(self.proj_ready, 1)

                        def values(g):
                            pe.wait_ge(self.v_copied, 4 * n + (g - 1 if g >= 2 else 0))
                            for t in range(4 * g, 4 * g + 4):
                                b, t0 = t // TB, (t % TB) * P
                                mm = pe.matmul(bank[6 + g % 2][:, (t % 4) * P:(t % 4 + 1) * P],
                                               hT[:, b, t0:t0 + P], wc[:, 4, :], start=True, stop=True)
                            mm.then_inc(self.v_ready, 1)

                        def norms(g):
                            pe.wait_ge(self.nln_done, 8 * n + 2 * g)
                            for qk in range(2):
                                pe.wait_ge(self.sq_ready, 8 * n + 2 * g + qk + 1)
                                pe.matmul(bank[4 + qk][:, :], headw[:, :], lns[:, qk, :], start=True, stop=True)\
                                    .then_inc(self.norm_ready, 1)

                        def scores(t):
                            w = keys_of(t)
                            last_q = (t * P + w - 1) // GW
                            pe.wait_ge(self.qk_done, 12 * n + 3 * (last_q + 1))
                            if t >= 2:
                                pe.wait_ge(self.exp_done, 16 * n + t - 1)
                            else:
                                pe.wait_ge(self.ab_done, 16 * n + 16)
                            o = bank[t % 2][:, 0:2 * w].rearrange("p (h q) -> p h q", h=2)
                            pe.matmul(o, kk[:, t // TB, (t % TB) * P:(t % TB + 1) * P], qm[:, :, t * P:t * P + w],
                                      start=True, stop=False)
                            pe.matmul(o, identb[:, :], maskb[:, :, 0:w], start=False, stop=True)\
                                .then_inc(self.sim_ready, 1)

                        def attend(t):
                            w, g, j = keys_of(t), t // 4, t % 4
                            pe.wait_ge(self.exp_done, 16 * n + t + 1)
                            pe.wait_ge(self.v_copied, 4 * n + g + 1)
                            if t == 0:
                                pe.wait_ge(self.nln_done, 8 * n + 8)
                            if t == TB:
                                pe.wait_ge(self.o_done, 8 * n + 2)
                            spill = j == 3 and w == BAND
                            if spill and g >= 1:
                                pe.wait_ge(self.o_done, 8 * n + 2 * g)
                            for h in range(2):
                                first = min(w, GW - j * P)
                                mm = pe.matmul(bank[2 + 2 * h + g % 2][:, j * P:j * P + first], vc[:, t, h, :],
                                               pt[:, t % 3, h, 0:first], start=t % TB == 0, stop=j == 3,
                                               skip_group_check=True)
                                if spill:
                                    mm = pe.matmul(bank[2 + 2 * h + (g + 1) % 2][:, 0:w - first], vc[:, t, h, :],
                                                   pt[:, t % 3, h, first:w], start=True, stop=False,
                                                   skip_group_check=True)
                            mm.then_inc(self.pv_ready, 1)

                        project(0)
                        for g in range(NG):
                            if g + 1 < NG:
                                values(g)
                                project(g + 1)
                            norms(g)
                        values(NG - 1)
                        scores(0)
                        for t in range(NT):
                            if t + 1 < NT:
                                scores(t + 1)
                            attend(t)
                    pe.wait_ge(self.wl_loaded, 16 * l + 16)
                    pe.wait_ge(self.o_done, 8 * CH * (l + 1))
                    pe.wait_ge(self.exp_done, 16 * CH * (l + 1))
                    for g in range(NG):
                        for c in range(CH):
                            mm = pe.matmul(bank[g][:, :], wl_o[:, c, :], oT[:, c, g * GW:(g + 1) * GW],
                                           start=c == 0, stop=c == CH - 1)
                        mm.then_inc(self.wo_ready, 1)
                    pe.wait_ge(self.shifted, 4 * l + 4)
                    self.ln1.pe(pe, l)
                    pe.wait_ge(self.ln1.normed, 8 * l + 8)

                    def hidden(g):
                        for j in range(HC):
                            if g > 0:
                                pe.wait_ge(self.gelu_done, HC * (NG * l + g - 1) + j + 1)
                            pe.matmul(bank[3 + j][:, :], wl_1[:, HC + j, :], group(kk, g), start=True, stop=True)\
                                .then_inc(self.hid_ready, 1)
                        for j in range(HC):
                            if g > 0:
                                pe.wait_ge(self.u_done, HC * (NG * l + g - 1) + j + 1)
                            pe.matmul(bank[j][:, :], wl_1[:, j, :], group(kk, g), start=True, stop=True)\
                                .then_inc(self.hid_ready, 1)

                    def outer(g):
                        pe.wait_ge(self.u_done, HC * (NG * l + g + 1))
                        pe.wait_ge(self.out_added, NG * l + (g - 1 if g >= 2 else 0))
                        for j in range(HC):
                            mm = pe.matmul(bank[6 + g % 2][:, :], wl_2[:, j, :], uh[:, j, :], start=j == 0,
                                           stop=j == HC - 1)
                        mm.then_inc(self.out_ready, 1)

                    for g in range(NG):
                        hidden(g)
                        outer(g)
                    layer_gate(pe, l - k * DEPTH)
                end_layers(pe)

            def act(self, a, k):
                ln_x.act(a, 1 + 2 * k)
                with a.Fori(k * DEPTH, (k + 1) * DEPTH) as l:
                    with a.Fori(0, CH) as c:
                        n = l * CH + c

                        def squares(g):
                            for qk in range(2):
                                a.wait_ge(self.proj_ready, 16 * n + 4 * g + 2 * qk + 2)
                                a.wait_ge(self.norm_ready, 8 * n + (2 * g - 1 + qk if g else 0))
                                a.activation(lns[:, qk, :], bank[2 * qk][:, :], ACT.Square).then_inc(self.sq_ready, 1)

                        def inverses(g):
                            a.wait_ge(self.qk_done, 12 * n + (3 * (g - 1) if g >= 2 else 0))
                            for qk in range(2):
                                a.wait_ge(self.norm_ready, 8 * n + 2 * g + qk + 1)
                                a.activation(rv[:, g % 2, qk, :], bank[4 + qk][:, :], ACT.Ln, bias=cols[:, 1:2],
                                             scale=NORM_SCALE).then_inc(self.nln_done, 1)
                            a.wait_ge(self.nln_done, 8 * n + 2 * g + 2)
                            a.activation(rv[:, g % 2, :, :], rv[:, g % 2, :, :], ACT.Exp, bias=cols[:, 2:3],
                                         scale=-0.5).then_inc(self.rinv_ready, 1)

                        def values(g):
                            a.wait_ge(self.v_ready, 4 * n + g + 1)
                            v4 = vc[:, 4 * g:4 * g + 4, :, :].rearrange("p t h (x d) -> p t (h x) d", d=DH)
                            a.activation(v4[:, :, 0:4:3, :],
                                         bank[6 + g % 2][:, :].rearrange("p (t h d) -> p t h d", t=4, h=2),
                                         ACT.Copy).then_inc(self.v_copied, 1)

                        def inverse_sums(g):
                            a.wait_ge(self.pv_ready, 16 * n + 4 * g + 4)
                            a.wait_ge(self.o_done, 8 * n + (2 * (g - 1) if g >= 2 else 0))
                            for h in range(2):
                                num, den = slice(h * DH, (h + 1) * DH), slice((1 - h) * DH, (2 - h) * DH)
                                a.activation(rd[num, g % 2, :], bank[2 + 2 * h + g % 2][den, :], ACT.Ln)\
                                    .then_inc(self.rd_done, 1)
                            a.wait_ge(self.rd_done, 12 * n + 3 * g + 2)
                            a.activation(rd[:, g % 2, :], rd[:, g % 2, :], ACT.Exp, scale=-1.0)\
                                .then_inc(self.rd_done, 1)

                        squares(0)
                        for g in range(NG):
                            if g + 1 < NG:
                                values(g)
                                squares(g + 1)
                            inverses(g)
                        values(NG - 1)
                        for t in range(NT):
                            w = keys_of(t)
                            a.wait_ge(self.sim_ready, 16 * n + t + 1)
                            a.wait_ge(self.pv_ready, 16 * n + (t - 2 if t >= 3 else 0))
                            a.activation(pt[:, t % 3, :, 0:w],
                                         bank[t % 2][:, 0:2 * w].rearrange("p (h q) -> p h q", h=2), ACT.Exp,
                                         scale=8.0).then_inc(self.exp_done, 1)
                            if t >= 5 and t % 4 == 1:
                                inverse_sums(t // 4 - 1)
                        inverse_sums(NG - 1)
                    self.ln1.act(a, l)
                    for g in range(NG):
                        for j in range(HC):
                            a.wait_ge(self.hid_ready, 2 * HC * (NG * l + g) + j + 1)
                            a.wait_ge(self.u_done, HC * (NG * l + g - 1) + j + 1 if g else HC * NG * l)
                            a.activation(gl[:, j, :], bank[3 + j][:, :], ACT.Gelu,
                                         bias=vec[:, V_B1 + HC + j:V_B1 + HC + j + 1]).then_inc(self.gelu_done, 1)
                    a.preload_act_table_set(LN_EXP)
                    layer_gate(a, l - k * DEPTH)
                end_layers(a)

            def dve(self, v, k):
                ln_x.dve(v, 1 + 2 * k)
                v.wait_ge(ln_x.normed, NG * (2 + 2 * k))

                def shift():
                    v.tensor_copy(hT[0:DH, :, 0:S], nT[0:DH, :, :]).then_inc(self.shifted, 1)
                    v.tensor_copy(hT[DH:P, :, 1:S + 1], nT[DH:P, :, :]).then_inc(self.shifted, 1)

                v.wait_ge(self.preset, 5 * k + 5)
                v.wait_ge(self.tab_loaded, 32 * k + 32)
                with v.Fori(k * DEPTH, (k + 1) * DEPTH) as l:
                    shift()
                    with v.Fori(0, CH) as c:
                        n = l * CH + c

                        def turn(g):
                            t0 = (g % GB) * GW
                            v.wait_ge(self.add_done, 8 * n + (2 * (g - 1) if g >= 2 else 0))
                            for j, (w, bk) in enumerate(((1, 1), (0, 0), (3, 3), (2, 2))):
                                v.wait_ge(self.proj_ready, 16 * n + 4 * g + j + 1)
                                if j % 2:
                                    v.wait_ge(self.sq_ready, 8 * n + 2 * g + j // 2 + 1)
                                v.scalar_tensor_tensor(ab[:, g % 2, j, :], bank[bk][:, :], vec[:, w:w + 1],
                                                       rot[:, w, t0:t0 + GW], ALU.mult, ALU.mult)\
                                    .then_inc(self.ab_done, 1)

                        def normalise(g):
                            v.wait_ge(self.rinv_ready, 4 * n + g + 1)
                            v.wait_ge(self.add_done, 8 * n + 2 * g + 2)
                            if g == 0:
                                v.wait_ge(self.sim_ready, 16 * n)
                            for h in range(2):
                                r = slice(h * DH, (h + 1) * DH)
                                v.scalar_tensor_tensor(qm[r, h, g * GW:(g + 1) * GW], rv[r, g % 2, 0, :], 1e12,
                                                       cq[r, g % 2, 0, :], ALU.min, ALU.mult).then_inc(self.qk_done, 1)
                            v.scalar_tensor_tensor(group(kk, g), rv[:, g % 2, 1, :], 1e12, cq[:, g % 2, 1, :],
                                                   ALU.min, ALU.mult).then_inc(self.qk_done, 1)

                        v.wait_ge(self.wq_loaded, 32 * l + 32)
                        turn(0)
                        for g in range(NG):
                            if g + 1 < NG:
                                turn(g + 1)
                            normalise(g)
                        for g in range(NG):
                            v.wait_ge(self.pv_ready, 16 * n + 4 * g + 4)
                            for h in range(2):
                                num, bk = slice(h * DH, (h + 1) * DH), bank[2 + 2 * h + g % 2]
                                v.wait_ge(self.rd_done, 12 * n + 3 * g + 3)
                                v.tensor_tensor(oT[num, ds(c, 1), g * GW:(g + 1) * GW].rearrange("p a t -> p (a t)"),
                                                bk[num, :], rd[num, g % 2, :], ALU.mult).then_inc(self.o_done, 1)
                    for g in range(NG):
                        v.wait_ge(self.wo_ready, NG * l + g + 1)
                        v.tensor_tensor(group(nT, g), group(nT, g), bank[g][:, :], ALU.add).then_inc(self.wo_added, 1)
                    v.wait_ge(self.wo_added, NG * (l + 1))
                    shift()
                    v.wait_ge(self.shifted, 4 * l + 4)
                    self.ln1.dve(v, l, vec[:, V_G:V_G + 1], vec[:, V_B:V_B + 1])
                    for g in range(NG):
                        for j in range(HC):
                            v.wait_ge(self.hid_ready, 2 * HC * (NG * l + g) + HC + j + 1)
                            v.wait_ge(self.gelu_done, HC * (NG * l + g) + j + 1)
                            v.wait_ge(self.out_ready, NG * l + g)
                            v.scalar_tensor_tensor(uh[:, j, :], bank[j][:, :], vec[:, V_B1 + j:V_B1 + j + 1],
                                                   gl[:, j, :], ALU.add, ALU.mult).then_inc(self.u_done, 1)
                        v.wait_ge(self.out_ready, NG * l + g + 1)
                        v.scalar_tensor_tensor(group(nT, g), bank[6 + g % 2][:, :], vec[:, V_B2:V_B2 + 1],
                                               group(nT, g), ALU.add, ALU.add).then_inc(self.out_added, 1)
                    layer_gate(v, l - k * DEPTH)
                end_layers(v)
                v.tensor_tensor(xT[:, :, :], xT[:, :, :], nT[:, :, :], ALU.add)

        def layer_gate(eng, l):
            g = gates[eng.engine]
            eng.drain().then_inc(stage_done, 1)
            eng.wait_ge(stage_done, 4 * l + 4 * (g.n + 1))

        def end_layers(eng):
            gates[eng.engine].n += DEPTH

        tf = Transformer("tf")

        scale7 = float(DH) ** -0.5

        per_pass = {k: sem("c_" + k) for k in (
            "v_ready v_copied proj_ready mt_psum mt_ready negm_ready").split()}

        mneg_loaded = [sem("c_mneg_loaded%d" % b) for b in range(B)]

        class Causal:
            def __init__(self, name, npairs, nh, scale, bias):
                self.name, self.np, self.nh, self.scale, self.bias = name, npairs, nh, scale, bias
                (self.kk, self.qm, self.kb, self.qb, self.vc, self.oT, self.w, self.wc, self.wp, self.pt,
                 self.rd, self.mx, self.negm, self.mt, self.cmask, self.bm,
                 self.vrow, self.tab, self.bp, self.bmc) = scope(*[(name + "_" + k[0],) + k[1:] for k in (
                     ("kk", [P, nh, B * S]), ("qm", [P, nh, B * S]), ("kb", [P, B * S], BF16),
                     ("qb", [P, nh, B * S], BF16), ("vc", [P, NT, 2, P]), ("oT", [P, npairs, B * S]),
                     ("w", [P, 3, npairs * P]), ("wc", [P, 3, P]), ("wp", [P, npairs, P]), ("pt", [P, 4, GW]),
                     ("rd", [P, 2, GW]), ("mx", [P, B * nh * TB]),
                     ("negm", [P, B * nh * TB], BF16), ("mt", [P, B, P]), ("cmask", [P, 3, P], BF16),
                     ("bm", [P, 2, 2 * npairs, NEAR], BF16),
                     ("vrow", [2 * npairs, P + NEAR]),
                     ("tab", [2 * npairs, REL + 1]), ("bp", [P, 1]),
                     ("bmc", [P, 2, 2, NEAR], BF16))])
                self.bmf = None if not bias else self.oT[:, 0:2, :].rearrange("p a t -> p (a t)")[
                    :, 0:2 * npairs * NEAR].rearrange("p (h q) -> p h q", q=NEAR)
                self.call = LN_CALLS[name]
                self.before = 1 if bias else 0
                self.loaded = sem(name + "_loaded")
                self.tab_loaded = sem(name + "_tab_loaded") if bias else None
                self.vrow_set = sem(name + "_vrow_set") if bias else None
                self.vrow_stored = sem(name + "_vrow_stored") if bias else None
                self.bmf_loaded = sem(name + "_bmf_loaded") if bias else None
                self.preset = sem(name + "_preset")
                self.v_ready = per_pass["v_ready"]
                self.wc_ready = sem(name + "_wc_ready") if npairs > 1 else None
                self.evacuated = sem(name + "_evacuated")
                self.half0 = sem(name + "_half0")
                self.half1 = sem(name + "_half1")
                self.exp_done = sem(name + "_exp_done")
                self.o_done = sem(name + "_o_done")
                self.proj_ready = per_pass["proj_ready"]
                self.v_copied = per_pass["v_copied"]
                self.max_done = sem(name + "_max_done")
                self.row_ready = sem(name + "_row_ready")
                self.negm_ready = per_pass["negm_ready"]
                self.mt_psum = per_pass["mt_psum"]
                self.mt_ready = per_pass["mt_ready"]
                self.mneg_loaded = mneg_loaded
                self.pv_ready = sem(name + "_pv_ready")
                self.score_ready = sem(name + "_score_ready")
                self.out_ready = sem(name + "_out_ready")
                self.rd_done = sem(name + "_rd_done")
                self.bm_ready = sem(name + "_bm_ready") if bias else None
                self.bmc_ready = sem(name + "_bmc_ready") if bias else None
                self.rows = [slice(h * DH, (h + 1) * DH) for h in range(nh)]
                self.extra = [slice((1 - h) * DH, (1 - h) * DH + 1) for h in range(nh)]

            def steps(self):
                out, unit = [], 0
                for b in range(B):
                    for h in range(self.nh):
                        for half in range(GB):
                            for j in range(4 * (half + 1)):
                                out.append((unit, b, h, half, j, max(j * P, half * GW), (half + 1) * GW))
                            unit += 1
                return out

            def loop(self, eng):
                return eng.Fori(0, self.np) if self.np > 1 else ExitStack()

            def sp(self, sp):
                name = self.name
                for dst, src in ((self.w[:, :, :], "w"), (self.wp[:, :, :], "wp"), (self.bp[:, :], "bp")):
                    sp.dma_start(dst, ins[name + "_" + src]).then_inc(self.loaded, 16)
                sp.dma_start(self.cmask[:, :, :], ins["cmask"]).then_inc(self.loaded, 16)
                if self.bias:
                    sp.dma_start(self.tab[:, :], ins[name + "_tab"]).then_inc(self.tab_loaded, 16)
                    sp.wait_ge(self.vrow_set, 3)
                    sp.dma_start(bias_rows, self.vrow[:, :]).then_inc(self.vrow_stored, 16)
                    sp.wait_ge(self.vrow_stored, 16)
                    for h in range(2 * self.np):
                        src = bass.AP(bias_rows.tensor, h * (P + NEAR), [[1, P], [1, NEAR]])
                        sp.dma_start(self.bmf[:, h, :], src).then_inc(self.bmf_loaded, 16)
                with self.loop(sp) as c:
                    n = 0 if self.np == 1 else c
                    m = n + self.before
                    for b in range(B):
                        sp.wait_ge(self.mt_ready, 2 * m + b + 1)
                        for h in range(self.nh):
                            sp.dma_start(self.qm[self.extra[h], h, b * S:(b + 1) * S].rearrange("p (i t) -> p i t", t=P),
                                         self.mt[h * TB:(h + 1) * TB, b, :]).then_inc(self.mneg_loaded[b], 16)

            def pool(self, p):
                nh = self.nh
                for t in (self.qm, self.kk, self.qb, self.kb):
                    p.memset(t[tuple(slice(None) for _ in t.shape)], 0.0).then_inc(self.preset, 1)
                p.memset(self.vc[:, :, :, :], 1.0).then_inc(self.preset, 1)
                p.wait_ge(self.preset, 5)
                if self.bias:
                    p.memset(self.vrow[:, 0:P - 1], -1e29).then_inc(self.vrow_set, 1)
                    p.wait_ge(self.vrow_set, 1)
                    p.memset(self.vrow[:, P - 1 + REL:P + NEAR], 0.0).then_inc(self.vrow_set, 1)
                    p.wait_ge(self.vrow_set, 2)
                for h in range(nh):
                    p.memset(self.kk[self.extra[h], h, :], 1.0).then_inc(self.preset, 1)
                    p.wait_ge(self.preset, 6 + h)
                if nh == 1:
                    p.memset(self.oT[:, :, :], 0.0).then_inc(self.preset, 1)

                with self.loop(p) as c:
                    n = 0 if self.np == 1 else c
                    m = n + self.before
                    p.wait_ge(self.half1, 2 * nh * GB * n)
                    p.wait_ge(self.v_ready, 4 * m)
                    if self.np > 1:
                        p.wait_ge(self.loaded, 64)
                        p.tensor_copy(self.wc[:, :, :], self.w[:, :, ds(c * P, P)]).then_inc(self.wc_ready, 1)
                    for g in range(GB, NG):
                        p.wait_ge(self.evacuated, 2 * nh * (NG * n + g + 1))
                        for h in range(nh):
                            r, cols_ = self.rows[h], slice(g * GW, (g + 1) * GW)
                            if h:
                                p.wait_ge(self.half1, 2 * nh * (GB * n + g - GB) + 2 * h)
                            elif g > GB:
                                p.wait_ge(self.half1, 2 * nh * (GB * n + g - GB))
                            zero = cols[r, 3:4].to_broadcast([DH, GW])
                            p.tensor_tensor(self.qb[r, h, cols_], self.qm[r, h, cols_], zero, ALU.add).then_inc(self.half1, 1)
                            p.tensor_tensor(self.kb[r, cols_], self.kk[r, h, cols_], zero, ALU.add).then_inc(self.half1, 1)

            def pe(self, pe):
                nh, steps = self.nh, self.steps()
                units, ns, nr, ne = B * nh * GB, len(self.steps()), B * nh * TB, 2 * NG * self.nh
                ln_x.pe(pe, self.call)
                pe.wait_ge(self.loaded, 64)
                pe.wait_ge(ln_x.normed, NG * (self.call + 1))
                with self.loop(pe) as c:
                    n = 0 if self.np == 1 else c
                    m = n + self.before
                    wc = self.wc if self.np > 1 else self.w
                    if self.np > 1:
                        pe.wait_ge(self.wc_ready, n + 1)
                    def project(g, k, bk):
                        pe.matmul(bank[bk], wc[:, k, :], group(nT, g), start=True, stop=True)\
                            .then_inc(self.proj_ready, 1)

                    def values(g, bk):
                        for t in range(4 * g, 4 * g + 4):
                            mm = pe.matmul(bank[bk][:, (t % 4) * P:(t % 4 + 1) * P],
                                           nT[:, t // TB, (t % TB) * P:(t % TB + 1) * P], wc[:, 2, :],
                                           start=True, stop=True)
                        mm.then_inc(self.v_ready, 1)

                    def row(r):
                        b, h, i = r // (nh * TB), r // TB % nh, r % TB
                        if h == 0 and i % 4 == 0:
                            pe.wait_ge((self.half0, self.half1)[b], 2 * nh * (GB * n + i // 4 + 1))
                        if r >= 3:
                            pe.wait_ge(self.max_done, nr * n + r - 2)
                        q = self.qb[:, h, b * S + i * P:b * S + (i + 1) * P]
                        w = (i + 1) * P
                        for a in range(0, w, GW):
                            e = min(w, a + GW)
                            pe.matmul(bank[2 * (r % 3) + a // GW][:, 0:e - a], q, self.kb[:, b * S + a:b * S + e],
                                      start=True, stop=e < w, skip_group_check=True)
                        o = (w - P) % GW
                        pe.matmul(bank[2 * (r % 3) + (w - P) // GW][:, o:o + P], identb[:, :], self.cmask[:, 0, :],
                                  start=False, stop=True, skip_group_check=True).then_inc(self.row_ready, 1)

                    def turn_maxima(b):
                        pe.wait_ge(self.negm_ready, 2 * m + b + 1)
                        pe.transpose(bank[7][0:nr // 2, 0:P // 2].bitcast(BF16),
                                     self.negm[:, b * nr // 2:(b + 1) * nr // 2], identb[:, :]).then_inc(self.mt_psum, 1)

                    pe.wait_ge(self.exp_done, ns * n)
                    for g in range(GB):
                        for k in range(2):
                            project(g, k, 2 * g + k)
                    pe.wait_ge(self.o_done, units * n)
                    values(0, 6)
                    values(1, 7)
                    for r in range(nr):
                        if r == 2:
                            pe.wait_ge(self.v_copied, 4 * m + 1)
                            project(2, 0, 6)
                        if r == 4:
                            pe.wait_ge(self.v_copied, 4 * m + 2)
                            project(2, 1, 7)
                        if r == 5:
                            pe.wait_ge(self.evacuated, ne * n + 5 * nh)
                            project(3, 0, 6)
                        if r == 6:
                            pe.wait_ge(self.evacuated, ne * n + 6 * nh)
                            project(3, 1, 7)
                        if r == nr // 2:
                            pe.wait_ge(self.evacuated, ne * n + 8 * nh)
                            values(2, 6)
                        if r == nr // 2 + 2:
                            turn_maxima(0)
                        if r == nr // 2 + 4:
                            pe.wait_ge(self.v_copied, 4 * m + 3)
                            values(3, 6)
                        if r == 1:
                            pe.wait_ge(self.evacuated, ne * n + 4 * nh)
                        row(r)
                    pe.wait_ge(self.max_done, nr * (n + 1))
                    pe.wait_ge(self.preset, 5 + nh)
                    if self.bias:
                        pe.wait_ge(self.bmc_ready, n + 1)

                    def attend(s):
                        unit, b, h, half, j, q0, q1 = steps[s]
                        pe.wait_ge(self.exp_done, ns * n + s + 1)
                        pe.wait_ge(self.v_copied, 4 * m + 4)
                        if j == 0:
                            pe.wait_ge(self.o_done, units * n + max(unit - 3, 0))
                            if unit % 4 == 3:
                                pe.wait_ge(self.mt_ready, 2 * m + B)
                        mm = pe.matmul(bank[4 + unit % 4][:, q0 - half * GW:q1 - half * GW],
                                       self.vc[:, b * TB + j, h, :], self.pt[:, s % 4, 0:q1 - q0],
                                       start=j == 0, stop=j == 4 * (half + 1) - 1, skip_group_check=True)
                        mm.then_inc(self.pv_ready, 1)

                    for s, (unit, b, h, half, j, q0, q1) in enumerate(steps):
                        if s >= 4:
                            pe.wait_ge(self.exp_done, ns * n + s - 3)
                        if s in (0, ns // 2):
                            pe.wait_ge(self.mneg_loaded[b], 16 * (nh * (n + 1) + self.before))
                        o = bank[s % 4]
                        lo, hi = max(q0, j * P), min(q1, j * P + (NEAR if self.bias else P))
                        mm = pe.matmul(o[:, 0:q1 - q0], self.kk[:, h, b * S + j * P:b * S + (j + 1) * P],
                                       self.qm[:, h, b * S + q0:b * S + q1], start=True, stop=lo >= hi,
                                       skip_group_check=True)
                        if lo < hi:
                            if self.bias:
                                for part in range(2):
                                    mm = pe.matmul(o[:, lo - q0:hi - q0], self.cmask[:, 2, :],
                                                   self.bmc[:, part, h, lo - j * P:hi - j * P], start=False,
                                                   stop=part == 1, skip_group_check=True)
                            else:
                                mm = pe.matmul(o[:, lo - q0:hi - q0], identb[:, :], self.cmask[:, 1, lo - j * P:hi - j * P],
                                               start=False, stop=True, skip_group_check=True)
                        mm.then_inc(self.score_ready, 1)
                        if s >= 1:
                            attend(s - 1)
                        if s == 2:
                            turn_maxima(1)
                    attend(ns - 1)
                pe.wait_ge(self.o_done, units * self.np)
                pe.wait_ge(self.exp_done, ns * self.np)
                for g in range(NG):
                    for c in range(self.np):
                        mm = pe.matmul(bank[g], self.wp[:, c, :], self.oT[:, c, g * GW:(g + 1) * GW],
                                       start=c == 0, stop=c == self.np - 1)
                    mm.then_inc(self.out_ready, 1)

            def act(self, a):
                nh, steps = self.nh, self.steps()
                units, ns, nr, ne = B * nh * GB, len(self.steps()), B * nh * TB, 2 * NG * self.nh
                last = {}
                for s, st in enumerate(steps):
                    last[st[0]] = s
                ln_x.act(a, self.call)
                a.wait_ge(self.preset, 2)
                with self.loop(a) as c:
                    n = 0 if self.np == 1 else c
                    m = n + self.before
                    def evacuate(g):
                        cols_ = slice(g * GW, (g + 1) * GW)
                        a.wait_ge((self.half0, self.half1)[g // GB], 2 * nh * GB * n)
                        for k, dst in enumerate((self.qm, self.kk)):
                            a.wait_ge(self.proj_ready, 2 * (NG * m + g) + 1 + k)
                            for h in range(nh):
                                bk = 2 * g + k if g < GB else 6 + k
                                a.activation(dst[self.rows[h], h, cols_], bank[bk][self.rows[h], :], ACT.Copy)\
                                    .then_inc(self.evacuated, 1)

                    def values(g, bk):
                        a.wait_ge(self.v_ready, NG * m + g + 1)
                        v4 = self.vc[:, 4 * g:4 * g + 4, :, :].rearrange("p t h (x d) -> p t (h x) d", d=DH)
                        a.activation(v4[:, :, 0:4:3, :], bank[bk].rearrange("p (t h d) -> p t h d", t=4, h=2),
                                     ACT.Copy).then_inc(self.v_copied, 1)

                    def turned_maxima(b):
                        a.wait_ge(self.mt_psum, 2 * m + b + 1)
                        a.wait_ge(self.mneg_loaded[b], 16 * (nh * n + self.before))
                        a.activation(self.mt[0:nr // 2, b, :], bank[7][0:nr // 2, 0:P // 2].bitcast(BF16), ACT.Copy)\
                            .then_inc(self.mt_ready, 1)

                    for g in range(GB):
                        evacuate(g)
                    a.wait_ge(self.preset, 5)
                    for g in range(GB):
                        values(g, 6 + g)
                    for g in range(GB, NG):
                        evacuate(g)
                    values(2, 6)
                    turned_maxima(0)
                    values(3, 6)

                    def inverse(unit):
                        h = unit // GB % nh
                        num, den = slice(h * DH, (h + 1) * DH), slice((1 - h) * DH, (2 - h) * DH)
                        a.wait_ge(self.pv_ready, ns * n + last[unit] + 1)
                        a.wait_ge(self.o_done, units * n + max(unit - 1, 0))
                        a.activation(self.rd[num, unit % 2, :], bank[4 + unit % 4][den, :], ACT.Ln)\
                            .then_inc(self.rd_done, 1)
                        a.wait_ge(self.rd_done, 2 * (units * n + unit) + 1)
                        a.activation(self.rd[num, unit % 2, :], self.rd[num, unit % 2, :], ACT.Exp, scale=-1.0)\
                            .then_inc(self.rd_done, 1)

                    due = {last[u] + 3: u for u in range(units)}
                    for s, (unit, b, h, half, j, q0, q1) in enumerate(steps):
                        a.wait_ge(self.score_ready, ns * n + s + 1)
                        a.wait_ge(self.pv_ready, ns * n + max(s - 3, 0))
                        a.activation(self.pt[:, s % 4, 0:q1 - q0], bank[s % 4][:, 0:q1 - q0], ACT.Exp,
                                     scale=self.scale).then_inc(self.exp_done, 1)
                        if s == 2:
                            turned_maxima(1)
                        if s in due:
                            inverse(due[s])
                    for s in sorted(due):
                        if s >= ns:
                            inverse(due[s])

            def dve(self, v):
                nh, steps = self.nh, self.steps()
                units, ns, nr = B * nh * GB, len(self.steps()), B * nh * TB
                last = {}
                for s, st in enumerate(steps):
                    last[st[0]] = s
                ln_x.dve(v, self.call)
                v.wait_ge(self.loaded, 64)
                if self.bias:
                    v.wait_ge(self.tab_loaded, 16)
                    v.wait_ge(self.vrow_set, 2)
                    v.tensor_scalar(self.vrow[:, P - 1:P - 1 + REL], self.tab[:, 0:REL], self.tab[:, REL:REL + 1],
                                    1.0 / self.scale, ALU.subtract, ALU.mult).then_inc(self.vrow_set, 1)
                    v.wait_ge(self.bmf_loaded, 16 * 2 * self.np)
                    v.tensor_copy(self.bm[:, 0, :, :], self.bmf[:, :, :]).then_inc(self.bm_ready, 1)
                    v.wait_ge(self.bm_ready, 1)
                    v.tensor_tensor(self.bm[:, 1, :, :], self.bmf[:, :, :], self.bm[:, 0, :, :], ALU.subtract)\
                        .then_inc(self.bm_ready, 1)
                    v.wait_ge(self.bm_ready, 2)
                with self.loop(v) as c:
                    n = 0 if self.np == 1 else c
                    m = n + self.before
                    if self.bias:
                        v.wait_ge(self.score_ready, ns * n)
                        v.tensor_copy(self.bmc[:, :, :, :], self.bm[:, :, ds(2 * c, 2), :]).then_inc(self.bmc_ready, 1)
                    v.wait_ge(self.preset, 5)
                    for g in range(GB):
                        v.wait_ge(self.evacuated, 2 * nh * (NG * n + g + 1))
                        for h in range(nh):
                            r, cols_ = self.rows[h], slice(g * GW, (g + 1) * GW)
                            v.tensor_copy(self.qb[r, h, cols_], self.qm[r, h, cols_]).then_inc(self.half0, 1)
                            v.tensor_copy(self.kb[r, cols_], self.kk[r, h, cols_]).then_inc(self.half0, 1)
                    for r in range(nr):
                        i = r % TB
                        v.wait_ge(self.row_ready, nr * n + r + 1)
                        v.tensor_reduce(self.mx[:, r:r + 1], ps[:, 2 * (r % 3):2 * (r % 3) + 2, :]
                                        .rearrange("p a b -> p (a b)")[:, 0:(i + 1) * P], AX_X, ALU.max)\
                            .then_inc(self.max_done, 1)
                        if i == TB - 1 and r // TB % nh == nh - 1:
                            b = r // (nh * TB)
                            v.wait_ge(self.max_done, nr * n + r + 1)
                            v.wait_ge(self.mt_psum, 2 * m)
                            v.tensor_scalar(self.negm[:, b * nr // 2:(b + 1) * nr // 2],
                                            self.mx[:, b * nr // 2:(b + 1) * nr // 2], -1.0, None, ALU.mult)\
                                .then_inc(self.negm_ready, 1)
                    if nh == 1:
                        v.wait_ge(self.preset, 7)
                    for unit in range(units):
                        b, h, half = unit // (nh * GB), unit // GB % nh, unit % GB
                        num = slice(h * DH, (h + 1) * DH)
                        v.wait_ge(self.rd_done, 2 * (units * n + unit) + 2)
                        dst = self.oT[num, ds(c, 1) if self.np > 1 else slice(0, 1), (b * GB + half) * GW:(b * GB + half + 1) * GW]
                        v.tensor_tensor(dst.rearrange("p a t -> p (a t)"), bank[4 + unit % 4][num, :],
                                        self.rd[num, unit % 2, :], ALU.mult).then_inc(self.o_done, 1)
                for g in range(NG):
                    v.wait_ge(self.out_ready, g + 1)
                    v.scalar_tensor_tensor(group(xT, g), bank[g], self.bp[:, 0:1], group(xT, g),
                                           ALU.add, ALU.add)

        class SignLinear:
            def __init__(self, name):
                self.w, self.vec, self.t = scope((name + "_w", [P, P]), (name + "_vec", [P, 2]),
                                                 (name + "_t", [P, NG, GW]))
                self.loaded, self.signed = sem(name + "_loaded"), sem(name + "_signed")
                self.ready, self.scaled = sem(name + "_ready"), sem(name + "_scaled")
                self.clipped = sem(name + "_clipped")

            def call(self, k):
                return 5 + 2 * k

            def sp(self, sp, k):
                sp.dma_start(self.w[:, :], ins["sl_w"]).then_inc(self.loaded, 16)
                sp.dma_start(self.vec[:, :], ins["sl_v"]).then_inc(self.loaded, 16)

            def pe(self, pe, k):
                ln_x.pe(pe, self.call(k))
                pe.wait_ge(self.signed, 2 * k + 2)
                pe.wait_ge(ln_x.normed, NG * (self.call(k) + 1))
                for g in range(NG):
                    pe.matmul(bank[g], self.w[:, :], group(nT, g), start=True, stop=True).then_inc(self.ready, 1)

            def act(self, a, k):
                ln_x.act(a, self.call(k))

            def pool(self, p, k):
                pass

            def dve(self, v, k):
                v.wait_ge(self.loaded, 32 * k + 32)
                v.tensor_scalar(self.w[:, :], self.w[:, :], 0.0, 2.0, ALU.is_ge, ALU.mult).then_inc(self.signed, 1)
                v.wait_ge(self.signed, 2 * k + 1)
                v.tensor_scalar(self.w[:, :], self.w[:, :], -1.0, None, ALU.add).then_inc(self.signed, 1)
                ln_x.dve(v, self.call(k))
                for g in range(NG):
                    v.wait_ge(self.ready, NG * k + g + 1)
                    v.tensor_scalar(self.t[:, g, :], bank[g], self.vec[:, 0:1], self.vec[:, 1:2], ALU.mult, ALU.add)\
                        .then_inc(self.scaled, 1)
                    v.wait_ge(self.scaled, NG * k + g + 1)
                    v.tensor_scalar(self.t[:, g, :], self.t[:, g, :], MAX_VAL, -MAX_VAL, ALU.min, ALU.max)\
                        .then_inc(self.clipped, 1)
                    v.wait_ge(self.clipped, NG * k + g + 1)
                    v.tensor_tensor(group(xT, g), group(xT, g), self.t[:, g, :], ALU.add)

        single = Causal("ca", 1, 1, 1.0, False)
        multi = Causal("cm", 8, 2, scale7, True)
        linear = SignLinear("sl")
        class Rope:
            NU = B * RH // 4
            NS = GB * TB
            NROW = 4 * TB * GB
            Q_TERMS = (0, 0, 1, 1, 0, 2)
            K_TERMS = (0, 1, 0, 1, 2, 0)

            def __init__(self):
                (self.w, self.wo, self.vec, self.bv, self.rt, self.pc, self.vall, self.vc, self.qs, self.ks,
                 self.zrow, self.pt, self.osb, self.rdn, self.on, self.sel, self.mx2, self.mx, self.negm,
                 self.mt) = scope(
                    ("ra_w", [P, 5, P]), ("ra_wo", [P, 4, P]), ("ra_vec", [P, 5]), ("ra_bv", [P, P]),
                    ("ra_rt", [P, 2, S]), ("ra_pc", [P, 6, B * S], BF16), ("ra_vall", [P, self.NU, TB, 32]),
                    ("ra_vc", [P, 2, TB, 4, 32]), ("ra_qs", [P, 2, 4, S], BF16), ("ra_ks", [P, 2, 4, S], BF16),
                    ("ra_zrow", [1, 4 * S], BF16), ("ra_pt", [P, 4, 2, GW]), ("ra_osb", [P, GB, GW]),
                    ("ra_rdn", [P, GB, GW]), ("ra_on", [P, self.NU, S]), ("ra_sel", [P, P]),
                    ("ra_mx2", [P, self.NROW]), ("ra_mx", [P, self.NROW // 2]),
                    ("ra_negm", [P, self.NROW // 2], BF16), ("ra_mt", [self.NROW // 2, P], BF16))
                self.ab = self.on[:, 0:4, :].rearrange("p a t -> p (a t)").rearrange("p (s j t) -> p s j t", s=2, j=4)
                self.f = self.on[:, 4:6, :].rearrange("p a t -> p (a t)").rearrange("p (s j t) -> p s j t", s=2, j=2)
                self.r = self.on[:, 6:8, :].rearrange("p a t -> p (a t)").rearrange("p (s j t) -> p s j t", s=2, j=2)
                self.loaded = sem("ra_loaded")
                self.parts_ready = sem("ra_parts_ready")
                self.parts_stored = sem("ra_parts_stored")
                self.preset = sem("ra_preset")
                self.ones_set = sem("ra_ones_set")
                self.unit_loaded = [sem("ra_unit_loaded%d" % par) for par in range(2)]
                self.mt_ready = sem("ra_mt_ready")
                self.maxima_loaded = sem("ra_maxima_loaded")
                self.pv_ready = sem("ra_pv_ready")
                self.rest_done = sem("ra_rest_done")
                self.ab_done = sem("ra_ab_done")
                self.added = sem("ra_added")
                self.v_ready = sem("ra_v_ready")
                self.vc_ready = sem("ra_vc_ready")
                self.proj_ready = sem("ra_proj_ready")
                self.v_psum = sem("ra_v_psum")
                self.max_done = sem("ra_max_done")
                self.row_ready = sem("ra_row_ready")
                self.negm_ready = sem("ra_negm_ready")
                self.ln_done = sem("ra_ln_done")
                self.mt_psum = sem("ra_mt_psum")
                self.exp_done = sem("ra_exp_done")
                self.o_copied = sem("ra_o_copied")
                self.sum_ready = sem("ra_sum_ready")
                self.score_ready = sem("ra_score_ready")
                self.on_done = sem("ra_on_done")
                self.out_ready = sem("ra_out_ready")
                self.rdn_ready = sem("ra_rdn_ready")
                self.mx_done = sem("ra_mx_done")

            def pipeline(self, eng, step):
                with eng.Fori(0, self.NU // 2 - 1) as it:
                    step(2 * it, 0, True)
                    step(2 * it + 1, 1, True)
                step(self.NU - 2, 0, True)
                step(self.NU - 1, 1, False)

            def load_unit(self, sp, u, par):
                for t in range(6):
                    for qk, dst in enumerate((self.qs, self.ks)):
                        part = (self.Q_TERMS, self.K_TERMS)[qk][t]
                        sp.dma_start(dst[8 * t:8 * t + 8, par, :, :],
                                     parts[qk * 3 + part, ds(u * 32, 32), :].rearrange("(h d) t -> d h t", d=8))\
                            .then_inc(self.unit_loaded[par], 16)
                sp.dma_start(self.qs[64:65, par, :, :].rearrange("p h t -> p (h t)"), self.zrow[:, :])\
                    .then_inc(self.unit_loaded[par], 16)

            def load_maxima(self, sp, u, par):
                sp.wait_ge(self.mt_ready, u + 1)
                sp.dma_start(self.qs[64:65, par, :, :].rearrange("p h (i t) -> p (h i) t", t=P), self.mt[:, :])\
                    .then_inc(self.maxima_loaded, 16)

            def sp(self, sp):
                for dst, src in ((self.w[:, :, :], "ra_w"), (self.wo[:, :, :], "ra_wo"), (self.vec[:, :], "ra_vec"),
                                 (self.rt[:, :, :], "ra_rt"), (self.sel[:, :], "ra_sel")):
                    sp.dma_start(dst, ins[src]).then_inc(self.loaded, 16)
                sp.dma_start(self.bv[:, :], ins["ra_bv"].partition_broadcast(P)).then_inc(self.loaded, 16)
                for b in range(B):
                    sp.wait_ge(self.parts_ready, 3 * GB * (b + 1))
                    sp.dma_start(parts[:, b * P:(b + 1) * P, :].rearrange("k r t -> r k t"),
                                 self.pc[:, :, b * S:(b + 1) * S]).then_inc(self.parts_stored, 16)
                sp.wait_ge(self.parts_stored, 16 * B)
                sp.wait_ge(self.preset, 5)
                for u in range(2):
                    self.load_unit(sp, u, u)
                self.load_maxima(sp, 0, 0)

                def step(u, par, more):
                    if more:
                        self.load_maxima(sp, u + 1, 1 - par)
                        if isinstance(u, int):
                            return
                        sp.wait_ge(self.pv_ready, self.NS * (u + 1))
                        self.load_unit(sp, u + 2, par)

                self.pipeline(sp, step)

            def pool(self, p):
                p.memset(self.qs[:, :, :, :], 0.0).then_inc(self.preset, 1)
                p.memset(self.ks[:, :, :, :], 0.0).then_inc(self.preset, 1)
                p.memset(self.vc[:, :, :, :, :], 0.0).then_inc(self.preset, 1)
                p.wait_ge(self.preset, 3)
                p.memset(self.vc[:, :, :, :, 8:9], 1.0).then_inc(self.preset, 1)
                p.memset(self.zrow[:, :], 0.0).then_inc(self.preset, 1)
                p.wait_ge(self.preset, 5)
                p.memset(self.ks[64:65, :, :, :], 1.0).then_inc(self.ones_set, 1)
                p.wait_ge(self.ones_set, 1)
                for g in range(NG):
                    p.wait_ge(self.rest_done, 2 * max(g - 1, 0))
                    p.wait_ge(self.parts_ready, 3 * max(g - 1, 0))
                    for qk in range(2):
                        p.wait_ge(self.ab_done, 4 * g + 2 * qk + 2)
                        p.tensor_tensor(self.f[:, g % 2, qk, :], self.ab[:, g % 2, 2 * qk, :],
                                        self.ab[:, g % 2, 2 * qk + 1, :], ALU.add).then_inc(self.added, 1)

                def values(u, par):
                    p.wait_ge(self.v_ready, B * TB)
                    p.tensor_copy(self.vc[:, par, :, :, 0:8], self.vall[:, ds(u, 1), :, :]
                                  .rearrange("p a j (h d) -> p (a j) h d", d=8)).then_inc(self.vc_ready, 1)

                values(0, 0)

                def step(u, par, more):
                    if more:
                        p.wait_ge(self.pv_ready, self.NS * u)
                        values(u + 1, 1 - par)

                self.pipeline(p, step)

            def row_bank(self, k):
                return bank[(4, 5, 7)[k % 3]]

            def piece(self, part, g):
                return self.pc[:, part:6:3, g * GW:(g + 1) * GW]

            def pe(self, pe):
                ln_x.pe(pe, LN_CALLS["ra"])
                pe.wait_ge(self.loaded, 96)
                pe.wait_ge(ln_x.normed, NG * (LN_CALLS["ra"] + 1))
                for g in range(NG):
                    for j in range(4):
                        if g > 0:
                            pe.wait_ge(self.ab_done, 4 * (g - 1) + j + 1)
                        pe.matmul(bank[j], self.w[:, j, :], group(nT, g), start=True, stop=True)\
                            .then_inc(self.proj_ready, 1)
                    if g >= 2:
                        pe.wait_ge(self.v_ready, 4 * (g - 1))
                    for t in range(4 * g, 4 * g + 4):
                        mm = pe.matmul(bank[4 + g % 2][:, (t % 4) * P:(t % 4 + 1) * P],
                                       nT[:, t // TB, (t % TB) * P:(t % TB + 1) * P], self.w[:, 4, :],
                                       start=True, stop=True)
                    mm.then_inc(self.v_psum, 1)
                pe.wait_ge(self.v_ready, NT)
                pe.wait_ge(self.ab_done, 4 * NG)

                def row(u, par, k):
                    h, i, half = k // (TB * GB), k // GB % TB, k % GB
                    if k == 0:
                        pe.wait_ge(self.unit_loaded[par], 8 * 13 * (u - par + 2))
                    pe.wait_ge(self.max_done, self.NROW * u + max(k - 2, 0))
                    if k == 2 and not (isinstance(u, int) and u == 0):
                        pe.wait_ge(self.ln_done, GB * (u - 1))
                    pe.matmul(self.row_bank(k), self.qs[:, par, h, i * P:(i + 1) * P],
                              self.ks[:, par, h, half * GW:(half + 1) * GW], start=True, stop=True)\
                        .then_inc(self.row_ready, 1)

                def maxima(u):
                    pe.wait_ge(self.negm_ready, u + 1)
                    pe.transpose(bank[7][0:self.NROW // 2, 0:P // 2].bitcast(BF16), self.negm[:, :], identb[:, :])\
                        .then_inc(self.mt_psum, 1)

                def step(u, par, more):
                    pe.wait_ge(self.maxima_loaded, 16 * (u + 1))
                    pe.wait_ge(self.vc_ready, u + 1)

                    def attend(s):
                        half, j = s // TB, s % TB
                        pe.wait_ge(self.exp_done, 2 * self.NS * u + 2 * s + 2)
                        if j == 0:
                            pe.wait_ge(self.o_copied, GB * u + half)
                        for h in range(4):
                            mm = pe.matmul(bank[6][32 * h:32 * h + 32, :], self.vc[:, par, j, h, :],
                                           self.pt[:, (2 * s + h // 2) % 4, h % 2, :], start=j == 0, stop=j == TB - 1,
                                           skip_group_check=True)
                            if h == 1 and more:
                                some_rows(s + 1, 3, 4)
                        mm.then_inc(self.pv_ready, 1)

                    def sums(half):
                        pe.wait_ge(self.o_copied, GB * u + half + 1)
                        pe.wait_ge(self.ln_done, GB * u + half)
                        if half == 0:
                            pe.wait_ge(self.mt_ready, u + 2 if more else u + 1)
                        pe.matmul(bank[7], self.sel[:, :], self.osb[:, half, :], start=True, stop=True)\
                            .then_inc(self.sum_ready, 1)

                    def some_rows(s, a, b):
                        k0, k1 = [self.NROW * max(x - 2, 0) // (self.NS - 4) for x in (s, s + 1)]
                        for k in range(k0 + a, min(k0 + b, k1, self.NROW)):
                            row(u + 1, 1 - par, k)

                    for s in range(self.NS):
                        half, j = s // TB, s % TB
                        for pair in range(2):
                            e = 2 * s + pair
                            pe.wait_ge(self.exp_done, 2 * self.NS * u + max(e - 1, 0))
                            for h in (2 * pair, 2 * pair + 1):
                                mm = pe.matmul(bank[h], self.ks[:, par, h, j * P:(j + 1) * P],
                                               self.qs[:, par, h, half * GW:(half + 1) * GW], start=True, stop=True)
                            mm.then_inc(self.score_ready, 1)
                            if more:
                                some_rows(s, pair, 1 + 2 * pair)
                        if s >= 1:
                            attend(s - 1)
                        if more:
                            some_rows(s, 4 if s >= 1 else 3, 6)
                            if s == self.NS - 2:
                                maxima(u + 1)
                        if s == self.NS - 1:
                            sums(0)
                    attend(self.NS - 1)
                    sums(1)

                for k in range(self.NROW):
                    row(0, 0, k)
                maxima(0)
                self.pipeline(pe, step)
                pe.wait_ge(self.on_done, GB * self.NU)
                for g in range(NG):
                    for c in range(4):
                        mm = pe.matmul(bank[g], self.wo[:, c, :],
                                       self.on[:, g // GB * 4 + c, (g % GB) * GW:(g % GB + 1) * GW],
                                       start=c == 0, stop=c == 3)
                    mm.then_inc(self.out_ready, 1)

            def act(self, a):
                ln_x.act(a, LN_CALLS["ra"])
                for g in range(NG):
                    for part in range(3):
                        if part == 0:
                            a.wait_ge(self.added, 2 * g + 2)
                        else:
                            a.wait_ge(self.rest_done, 2 * g + part)
                        src = self.f if part == 0 else self.r
                        a.activation(self.piece(part, g), src[:, g % 2, :, :], ACT.Copy).then_inc(self.parts_ready, 1)

                def maxima(u):
                    a.wait_ge(self.mt_psum, u + 1)
                    a.wait_ge(self.maxima_loaded, 16 * u)
                    a.activation(self.mt[:, :], bank[7][0:self.NROW // 2, 0:P // 2].bitcast(BF16), ACT.Copy)\
                        .then_inc(self.mt_ready, 1)

                def step(u, par, more):
                    def copy(half):
                        a.wait_ge(self.pv_ready, self.NS * u + TB * (half + 1))
                        a.wait_ge(self.on_done, GB * u)
                        a.activation(self.osb[:, half, :], bank[6], ACT.Copy).then_inc(self.o_copied, 1)

                    def inverse(half):
                        a.wait_ge(self.sum_ready, GB * u + half + 1)
                        a.activation(self.rdn[:, half, :], bank[7], ACT.Ln).then_inc(self.ln_done, 1)
                        a.wait_ge(self.ln_done, GB * u + half + 1)
                        a.activation(self.rdn[:, half, :], self.rdn[:, half, :], ACT.Exp, scale=-1.0)\
                            .then_inc(self.rdn_ready, 1)

                    for s in range(self.NS):
                        for pair in range(2):
                            e = 2 * s + pair
                            a.wait_ge(self.score_ready, 2 * self.NS * u + e + 1)
                            a.wait_ge(self.pv_ready, self.NS * u + max(s - 1, 0))
                            a.activation(self.pt[:, e % 4, :, :], ps[:, 2 * pair:2 * pair + 2, :], ACT.Exp,
                                         scale=float(RD) ** -0.5).then_inc(self.exp_done, 1)
                        if s == TB:
                            copy(0)
                        if more and s == self.NS - 2:
                            maxima(u + 1)
                    inverse(0)
                    copy(1)
                    inverse(1)

                maxima(0)
                self.pipeline(a, step)

            def dve(self, v):
                ln_x.dve(v, LN_CALLS["ra"])
                v.wait_ge(self.loaded, 96)

                def rest(g, part):
                    if g < 0:
                        return
                    v.wait_ge(self.parts_ready, 3 * g + part + 1)
                    v.wait_ge(self.added, 2 * g + 2)
                    v.wait_ge(self.rest_done, 2 * g + part)
                    src = self.f if part == 0 else self.r
                    v.tensor_tensor(self.r[:, g % 2, :, :], src[:, g % 2, :, :], self.piece(part, g), ALU.subtract)\
                        .then_inc(self.rest_done, 1)

                for g in range(NG):
                    t0 = (g % GB) * GW
                    v.wait_ge(self.added, 2 * max(g - 1, 0))
                    for j in range(4):
                        v.wait_ge(self.proj_ready, 4 * g + j + 1)
                        v.scalar_tensor_tensor(self.ab[:, g % 2, j, :], bank[j], self.vec[:, j:j + 1],
                                               self.rt[:, j % 2, t0:t0 + GW], ALU.add, ALU.mult)\
                            .then_inc(self.ab_done, 1)
                    rest(g - 1, 0)
                    v.wait_ge(self.v_psum, g + 1)
                    for t in range(4 * g, 4 * g + 4):
                        b, j = t // TB, t % TB
                        v.tensor_tensor(self.vall[:, 4 * b:4 * b + 4, j, :],
                                        bank[4 + g % 2][:, (t % 4) * P:(t % 4 + 1) * P].rearrange("p (u d) -> p u d", u=4),
                                        self.bv[:, :].rearrange("p (u d) -> p u d", u=4), ALU.add)\
                            .then_inc(self.v_ready, 1)
                    rest(g - 1, 1)
                for part in range(2):
                    rest(NG - 1, part)

                def rows(u, k0, k1):
                    for k in range(k0, k1):
                        v.wait_ge(self.row_ready, self.NROW * u + k + 1)
                        v.tensor_reduce(self.mx2[:, k:k + 1], self.row_bank(k), AX_X, ALU.max).then_inc(self.max_done, 1)

                def maxima(u):
                    v.wait_ge(self.max_done, self.NROW * (u + 1))
                    v.tensor_reduce(self.mx[:, :], self.mx2[:, :].rearrange("p (r a) -> p r a", a=GB), AX_X, ALU.max)\
                        .then_inc(self.mx_done, 1)
                    v.wait_ge(self.mx_done, u + 1)
                    v.wait_ge(self.mt_psum, u)
                    v.tensor_scalar(self.negm[:, :], self.mx[:, :], -1.0, None, ALU.mult).then_inc(self.negm_ready, 1)

                def step(u, par, more):
                    def output(half):
                        v.wait_ge(self.rdn_ready, GB * u + half + 1)
                        v.tensor_tensor(self.on[:, ds(u, 1), half * GW:(half + 1) * GW].rearrange("p a t -> p (a t)"),
                                        self.osb[:, half, :], self.rdn[:, half, :], ALU.mult).then_inc(self.on_done, 1)

                    if more:
                        rows(u + 1, 0, self.NROW)
                        maxima(u + 1)
                    output(0)
                    output(1)

                v.wait_ge(self.rest_done, 2 * NG)
                v.wait_ge(self.parts_ready, 3 * NG)
                rows(0, 0, self.NROW)
                maxima(0)
                self.pipeline(v, step)
                for g in range(NG):
                    v.wait_ge(self.out_ready, g + 1)
                    v.scalar_tensor_tensor(group(xT, g), bank[g], self.vec[:, 4:5], group(xT, g),
                                           ALU.add, ALU.add)

        rope = Rope()


        yout, = scope(("yout", [P, NT, P]))
        oxpose_ready, oxpose_used = sem("oxpose_ready"), sem("oxpose_used")

        def store_pe(pe):
            for t in range(NT):
                mm = pe.transpose(bank[t // 4][:, (t % 4) * P:(t % 4 + 1) * P],
                                  xT[:, t // TB, (t % TB) * P:(t % TB + 1) * P], ident[:, :])
                if t % 4 == 3:
                    mm.then_inc(oxpose_ready, 1)

        def store_dve(v):
            for g in range(NG):
                v.wait_ge(oxpose_ready, g + 1)
                v.tensor_copy(yout[:, 4 * g:4 * g + 4, :], bank[g][:, :].rearrange("p (t f) -> p t f", t=4))\
                    .then_inc(oxpose_used, 1)

        def store_sp(sp):
            for g in range(NG):
                sp.wait_ge(oxpose_used, g + 1)
                sp.dma_start(out.rearrange("b (t p) f -> p (b t) f", p=P)[:, 4 * g:4 * g + 4, :],
                             yout[:, 4 * g:4 * g + 4, :]).then_inc(stored, 16)
            sp.wait_ge(stored, 16 * NG)

        STAGES = ((mamba, ()), (tf, (0,)), (single, ()), (tf, (1,)), (rope, ()), (linear, (0,)), (multi, ()),
                  (linear, (1,)))

        block = ctx.enter_context(nc.Block())

        @block.sync
        def _(sp):
            n = 0
            load_sp(sp)
            for stage, call in STAGES[:last]:
                n += 1
                sp.wait_ge(stage_done, 4 * n)
                if stage is tf:
                    stage.sp(sp, n, *call)
                    n += DEPTH
                else:
                    stage.sp(sp, *call)
            sp.wait_ge(stage_done, 4 * (n + 1))
            store_sp(sp)

        @block.tensor
        def _(eng):
            load_pe(eng)
            gate(eng)
            for stage, call in STAGES[:last]:
                stage.pe(eng, *call)
                gate(eng)
            store_pe(eng)

        @block.scalar
        def _(eng):
            load_act(eng)
            gate(eng)
            for stage, call in STAGES[:last]:
                stage.act(eng, *call)
                gate(eng)

        @block.vector
        def _(eng):
            load_dve(eng)
            gate(eng)
            for stage, call in STAGES[:last]:
                stage.dve(eng, *call)
                gate(eng)
            store_dve(eng)

        @block.gpsimd
        def _(eng):
            load_pool(eng)
            gate(eng)
            for stage, call in STAGES[:last]:
                stage.pool(eng, *call)
                gate(eng)


def constants():
    t = np.arange(P)
    q = np.zeros((P, NL + 3, P), np.float32)
    m_ = np.zeros((P, NL + 1, P), np.float32)
    for n, m in enumerate(LEVELS):
        pair = t // (2 * m)
        upper = (t // m) % 2 == 1
        r = pair * 2 * m + m
        for j in range(P):
            if upper[j]:
                q[r[j]:j + 1, n, j] = 1.0
            else:
                q[j + 1:r[j], n, j] = 1.0
        m_[:, n, :] = (pair[:, None] == pair[None, :]) & ~upper[:, None] & upper[None, :]
    m_[:, NL, :] = np.eye(P)
    q[:, Q_IN, :] = t[:, None] <= t[None, :]
    q[:, Q_END, :] = t[:, None] > t[None, :]
    q[:, Q_ALL, :] = 1.0
    heads = np.kron(np.eye(P // DH), np.ones((DH, DH))).astype(np.float32)
    return {"rot": rotary(), "maskb": band_mask(), "cmask": causal_masks(), "ra_rt": rope_tables(),
            "ra_sel": sum_selector(), "ident": np.eye(P, dtype=np.float32), "identb": np.eye(P).astype(mybir.dt.np(BF16)),
            "meanw": np.full((P, P), 1.0 / P, np.float32), "headw": heads, "qmat": q, "gmask": m_}


def rotary():
    f32 = np.float32
    half = np.arange(0, DH, 2, dtype=f32)
    inv = (f32(1.0) / f32(10000.0) ** (half / f32(DH))).astype(f32)
    t = np.arange(S, dtype=f32)
    freqs = (t[:, None] * inv[None, :]).astype(f32)
    base = (half + f32(0.4 * DH)) / f32(1.4 * DH)
    power = (t - S // 2) / f32(WINDOW // 2)
    scale = base[None, :].astype(np.float64) ** power[:, None].astype(np.float64)
    two = lambda a, sign=1.0: np.tile(np.concatenate([sign * a, a], 1).T, (2, 1))
    c, s_ = np.cos(freqs.astype(np.float64)), np.sin(freqs.astype(np.float64))
    return np.stack([two(c * scale), two(s_ * scale, -1.0), two(c / scale), two(s_ / scale, -1.0)], 1).astype(f32)


def band_mask():
    d = np.arange(BAND)[None, :] - np.arange(P)[:, None]
    m = np.where((d >= 0) & (d <= WINDOW), 0.0, -1e30)
    return np.stack([m, m], 1).astype(mybir.dt.np(BF16))


def rope_tables():
    f32 = np.float32
    inv = (f32(1.0) / f32(10000.0) ** (np.arange(0, RD, 2, dtype=f32) / f32(RD))).astype(f32)
    freqs = (np.arange(S, dtype=f32)[:, None] * inv[None, :]).astype(f32).astype(np.float64)
    sign = np.tile([-1.0, 1.0], RD // 2)
    rows = lambda a: np.tile(np.repeat(a, 2, axis=1).T, (RH, 1))
    return np.stack([rows(np.cos(freqs)), rows(np.sin(freqs)) * np.tile(sign, RH)[:, None]], 1).astype(f32)


def sum_selector():
    r = np.arange(P)
    return ((r[:, None] // 32 == r[None, :] // 32) & (r[:, None] % 32 == RD)).astype(np.float32)


def causal_masks():
    d = np.arange(P)[:, None] - np.arange(P)[None, :]
    return np.stack([np.where(d >= 0, 0.0, -1e30), np.where(d <= 0, 0.0, -1e30), np.eye(P)[::-1]],
                    1).astype(mybir.dt.np(BF16))


def pack(a):
    f = lambda n: np.asarray(a[n])
    out = {"x": f("L0_attn_a_x"), "b_dt": f("L0_attn_a_b_dt")}
    dbc = np.concatenate([f("L0_attn_a_W_dt"), f("L0_attn_a_W_B"), f("L0_attn_a_W_C")], 1)
    vec = np.concatenate([f("L0_attn_a_conv_w")[:, 0, :], f("L0_attn_a_conv_b")[:, None], f("L0_attn_a_D")[:, None]], 1)
    halves = lambda w: w.reshape(HALVES, P, -1).transpose(1, 0, 2).reshape(P, -1)
    out["wm"] = np.concatenate([f("L0_attn_a_W_in"), halves(dbc), halves(f("L0_attn_a_W_out")), halves(vec)], 1)
    swap = np.arange(HEADS * DH).reshape(HEADS, 2, DH // 2)[:, ::-1].reshape(-1)
    layers = []
    for l in range(DEPTH):
        q, k, v = np.split(f("L0_ffn_wqkv")[l], 3, axis=1)
        wo = f("L0_ffn_wo")[l].reshape(CH, P, P).transpose(1, 0, 2).reshape(P, -1)
        pad = lambda w: np.pad(w, ((0, 0), (0, HC * P - HID)))
        w1 = np.concatenate([pad(w) for w in np.split(f("L0_ffn_w1")[l], 2, axis=1)], 1)
        w2 = pad(f("L0_ffn_w2")[l].T).T.reshape(HC, P, P).transpose(1, 0, 2).reshape(P, -1)
        b1 = np.concatenate([pad(w[None]).reshape(HC, P) for w in np.split(f("L0_ffn_b1")[l], 2)], 0).T
        two = lambda x: np.tile(x, 2)
        qs, ks = f("L0_ffn_q_scale")[l], f("L0_ffn_k_scale")[l]
        vecs = np.stack([two(qs), two(qs[swap[:DH]]), two(ks), two(ks[swap[:DH]])], 1)
        rest = np.stack([f("L0_ffn_ln_g")[l], f("L0_ffn_ln_b")[l], f("L0_ffn_b2")[l]], 1)
        layers.append(np.concatenate([q, q[:, swap], k, k[:, swap], v, wo, w1, w2, vecs, b1, rest], 1))
    out["wl"] = np.stack(layers)
    turn = np.arange(P).reshape(P // 2, 2)[:, ::-1].reshape(-1)
    wq, wk, wv = (f("L1_attn_a_W" + n).T for n in "qkv")
    bq, bk = f("L1_attn_a_bq"), f("L1_attn_a_bk")
    out["ra_w"] = np.stack([wq, wq[:, turn], wk, wk[:, turn], wv], 1)
    out["ra_vec"] = np.stack([bq, bq[turn], bk, bk[turn], f("L1_attn_a_bo")], 1)
    out["ra_bv"] = f("L1_attn_a_bv")
    wo = np.pad(f("L1_attn_a_Wo").T.reshape(4, 4, RD, P), ((0, 0), (0, 0), (0, 32 - RD), (0, 0)))
    out["ra_wo"] = wo.reshape(4, P, P).transpose(1, 0, 2)
    wide = lambda w: np.pad(w, ((0, 0), (0, P - w.shape[1])))
    out["ca_w"] = np.stack([wide(f("L0_attn_b_" + n)) for n in "QKV"], 1)
    out["ca_wp"] = wide(f("L0_attn_b_O")).T.reshape(1, P, P).transpose(1, 0, 2)
    out["ca_bp"] = np.zeros((P, 1), np.float32)
    out["cm_w"] = np.stack([f("L1_attn_b_" + n).transpose(1, 0, 2).reshape(P, -1) for n in ("Wq", "Wk", "Wv")], 1)
    out["cm_wp"] = f("L1_attn_b_Wp").reshape(8, P, P).transpose(1, 0, 2)
    out["cm_bp"] = f("L1_attn_b_bp")[:, None]
    out["cm_tab"] = f("L1_attn_b_rel_table")[REL::-1].T
    out["sl_w"] = f("L1_ffn_weights").T
    out["sl_v"] = np.stack([f("L1_ffn_scale"), f("L1_ffn_bias")], 1)
    return {k: np.ascontiguousarray(v) for k, v in out.items()}


def kernel(**inputs):
    import concourse.bacc as bacc
    from concourse.bass_utils import run_bass_kernel_spmd

    nc = bacc.Bacc("TRN2", target_bir_lowering=False, num_devices=1)
    arrays = {**pack(inputs), **constants()}
    ins = {n: nc.dram_tensor("in_" + n, a.shape, mybir.dt.from_np(a.dtype), kind="ExternalInput").ap() for n, a in arrays.items()}
    out = nc.dram_tensor("y", (B, S, P), F32, kind="ExternalOutput").ap()
    build(nc, ins, out)
    return run_bass_kernel_spmd(nc, [{"in_" + n: a for n, a in arrays.items()}], core_ids=[0]).results[0]["y"]
```
